# Optimizing a Trainium2 kernel written in Bass

```python
import numpy as np
import jax
import jax.numpy as jnp

def _softmax(x, axis=-1):
    return jax.nn.softmax(x, axis=axis)

def _gelu(x):
    return jax.nn.gelu(x, approximate=True)

def _silu(x):
    return jax.nn.silu(x)

def _sigmoid(x):
    return jax.nn.sigmoid(x)

def _layernorm(x, axis=-1, eps=1e-05):
    m = jnp.mean(x, axis=axis, keepdims=True)
    v = jnp.var(x, axis=axis, keepdims=True)
    return (x - m) / jnp.sqrt(v + eps)

def _scatter_add(tgt, idx, src, axis=0):
    return tgt.at[idx].add(src)

def _segment_sum(src, seg, n):
    return jax.ops.segment_sum(src, seg, n)
kernel_name = 'mk_perceiver_d1_seqx_r8_099cb9'

def setup_inputs(seed: int=0):
    np.random.seed(seed)
    _w = jnp.asarray

    def _rec_inputs():
        import jax
        import jax.numpy as jnp
        _rk = jax.random.key(seed)
        x = -0.0005207 + 1.001 * jax.random.normal(jax.random.fold_in(_rk, 1), (8, 32, 512), jnp.float32)
        _lenS = 32 - jax.random.randint(jax.random.fold_in(_rk, 7), (8,), 0, max(1, 32 // 4) + 1, jnp.int32)
        _lenS2 = 512 - jax.random.randint(jax.random.fold_in(_rk, 8), (8,), 0, max(1, 512 // 4) + 1, jnp.int32)
        _ctx_4096P = jax.random.normal(jax.random.fold_in(_rk, 11), (8, 16, 512), jnp.float32)
        _ctx_4096c = jax.random.dirichlet(jax.random.fold_in(_rk, 511), 0.3 * jnp.ones((16,), jnp.float32), (8, 512))
        _ctx_4096t = jnp.einsum('bsk,bkd->bsd', _ctx_4096c, _ctx_4096P)
        _ctx_4096t = _ctx_4096t * jax.lax.rsqrt(jnp.mean(jnp.square(_ctx_4096t)) + 1e-12) * 0.953939
        ctx_4096 = -0.00010331 + 0.999899 * (_ctx_4096t + 0.3 * jax.random.normal(jax.random.fold_in(_rk, 611), (8, 512, 512), jnp.float32))
        return (x, ctx_4096)
    x, ctx_4096 = _rec_inputs()

    def _L0_xattn_setup():
        import jax, jax.numpy as jnp
        import numpy as np
        B, Q, D = (8, 64, 512)
        CTX = 512
        H, KV, HD = (16, 4, 96)
        G = H // KV
        key = jax.random.key(seed)
        ks = jax.random.split(key, 6)
        s = 0.02
        return {'latents': jax.random.normal(ks[0], (B, Q, D), jnp.float32), 'context': jax.random.normal(ks[1], (B, CTX, D), jnp.float32), 'Wq': jax.random.normal(ks[2], (H * HD, D), jnp.float32) * s, 'Wk': jax.random.normal(ks[3], (KV * HD, D), jnp.float32) * s, 'Wv': jax.random.normal(ks[4], (KV * HD, D), jnp.float32) * s, 'Wo': jax.random.normal(ks[5], (D, H * HD), jnp.float32) * s}
    _L0_xattn_all = _L0_xattn_setup()
    _L0_xattn_in = {k: v for k, v in _L0_xattn_all.items() if k in ('Wq', 'Wk', 'Wv', 'Wo')}
    del _L0_xattn_all

    def _L0_attn_setup():
        import jax, jax.numpy as jnp
        import numpy as np
        B, S, H = (1, 256, 512)
        NH = 32
        QK_NOPE, QK_ROPE, V_DIM = (128, 64, 128)
        Q_LORA, KV_LORA = (192, 64)
        EPS = 1e-06

        def _rms_norm(x, w):
            return x * jax.lax.rsqrt(jnp.mean(x * x, axis=-1, keepdims=True) + EPS) * w

        def _rope_cos_sin(seqlen, dim):
            freqs = 1.0 / 10000.0 ** (jnp.arange(0, dim, 2, dtype=jnp.float32) / dim)
            t = jnp.arange(seqlen, dtype=jnp.float32)
            ang = jnp.outer(t, freqs)
            return (jnp.cos(ang), jnp.sin(ang))

        def _apply_rope(x, cos, sin):
            x1 = x[..., 0::2]
            x2 = x[..., 1::2]
            r1 = x1 * cos - x2 * sin
            r2 = x1 * sin + x2 * cos
            return jnp.stack([r1, r2], axis=-1).reshape(x.shape)
        key = jax.random.key(seed)
        ks = jax.random.split(key, 7)
        s = 0.02
        return {'x': jax.random.normal(ks[0], (B, S, H), jnp.float32), 'wq_a': jax.random.normal(ks[1], (Q_LORA, H), jnp.float32) * s, 'q_norm_w': jnp.ones((Q_LORA,), jnp.float32), 'wq_b': jax.random.normal(ks[2], (NH * (QK_NOPE + QK_ROPE), Q_LORA), jnp.float32) * s, 'wkv_a': jax.random.normal(ks[3], (KV_LORA + QK_ROPE, H), jnp.float32) * s, 'kv_norm_w': jnp.ones((KV_LORA,), jnp.float32), 'wkv_b': jax.random.normal(ks[4], (NH * (QK_NOPE + V_DIM), KV_LORA), jnp.float32) * s, 'wo': jax.random.normal(ks[5], (H, NH * V_DIM), jnp.float32) * s}
    _L0_attn_all = _L0_attn_setup()
    _L0_attn_in = {k: v for k, v in _L0_attn_all.items() if k in ('wq_a', 'q_norm_w', 'wq_b', 'wkv_a', 'kv_norm_w', 'wkv_b', 'wo')}
    del _L0_attn_all

    def _L0_ffn_setup():
        import jax, jax.numpy as jnp
        import numpy as np
        B, S, D_IN, D_OUT = (4, 256, 512, 512)
        key = jax.random.key(seed)
        k1, k2, k3 = jax.random.split(key, 3)
        input = jax.random.normal(k1, (B, S, D_IN), dtype=jnp.float16)
        weight = jax.random.normal(k2, (D_OUT, D_IN), dtype=jnp.float16) * jnp.float16(0.02)
        bias = jax.random.normal(k3, (1, D_OUT), dtype=jnp.float16)
        return {'input': input, 'weight': weight, 'bias': bias}
    _L0_ffn_all = _L0_ffn_setup()
    _L0_ffn_in = {k: v for k, v in _L0_ffn_all.items() if k in ('weight', 'bias')}
    del _L0_ffn_all
    return {'x': x, 'ctx_4096': ctx_4096, 'L0_xattn_Wq': _L0_xattn_in['Wq'], 'L0_xattn_Wk': _L0_xattn_in['Wk'], 'L0_xattn_Wv': _L0_xattn_in['Wv'], 'L0_xattn_Wo': _L0_xattn_in['Wo'], 'L0_attn_wq_a': _L0_attn_in['wq_a'], 'L0_attn_q_norm_w': _L0_attn_in['q_norm_w'], 'L0_attn_wq_b': _L0_attn_in['wq_b'], 'L0_attn_wkv_a': _L0_attn_in['wkv_a'], 'L0_attn_kv_norm_w': _L0_attn_in['kv_norm_w'], 'L0_attn_wkv_b': _L0_attn_in['wkv_b'], 'L0_attn_wo': _L0_attn_in['wo'], 'L0_ffn_weight': _L0_ffn_in['weight'], 'L0_ffn_bias': _L0_ffn_in['bias']}

def reference(x, ctx_4096, L0_xattn_Wq, L0_xattn_Wk, L0_xattn_Wv, L0_xattn_Wo, L0_attn_wq_a, L0_attn_q_norm_w, L0_attn_wq_b, L0_attn_wkv_a, L0_attn_kv_norm_w, L0_attn_wkv_b, L0_attn_wo, L0_ffn_weight, L0_ffn_bias):
    import jax
    import jax.numpy as jnp

    def _L0_xattn_ref(latents, context, Wq, Wk, Wv, Wo):
        import jax, jax.numpy as jnp
        import numpy as np
        B, Q, D = (8, 64, 512)
        CTX = 512
        H, KV, HD = (16, 4, 96)
        G = H // KV
        b, q_len, _ = latents.shape
        hidden = jnp.concatenate([context, latents], axis=1)
        s_len = hidden.shape[1]
        q = (latents @ Wq.T).reshape(b, q_len, H, HD)
        k = (hidden @ Wk.T).reshape(b, s_len, KV, HD)
        v = (hidden @ Wv.T).reshape(b, s_len, KV, HD)
        q = q.transpose(0, 2, 1, 3).reshape(b, KV, G, q_len, HD)
        k = k.transpose(0, 2, 1, 3)
        v = v.transpose(0, 2, 1, 3)
        scale = 1.0 / jnp.sqrt(jnp.asarray(HD, q.dtype))
        scores = jnp.einsum('bkgqd,bksd->bkgqs', q, k) * scale
        attn = jax.nn.softmax(scores.astype(jnp.float32), axis=-1).astype(q.dtype)
        out = jnp.einsum('bkgqs,bksd->bkgqd', attn, v)
        out = out.reshape(b, H, q_len, HD).transpose(0, 2, 1, 3).reshape(b, q_len, H * HD)
        return out @ Wo.T

    def _L0_attn_ref(x, wq_a, q_norm_w, wq_b, wkv_a, kv_norm_w, wkv_b, wo):
        import jax, jax.numpy as jnp
        import numpy as np
        B, S, H = (1, 256, 512)
        NH = 32
        QK_NOPE, QK_ROPE, V_DIM = (128, 64, 128)
        Q_LORA, KV_LORA = (192, 64)
        EPS = 1e-06

        def _rms_norm(x, w):
            return x * jax.lax.rsqrt(jnp.mean(x * x, axis=-1, keepdims=True) + EPS) * w

        def _rope_cos_sin(seqlen, dim):
            freqs = 1.0 / 10000.0 ** (jnp.arange(0, dim, 2, dtype=jnp.float32) / dim)
            t = jnp.arange(seqlen, dtype=jnp.float32)
            ang = jnp.outer(t, freqs)
            return (jnp.cos(ang), jnp.sin(ang))

        def _apply_rope(x, cos, sin):
            x1 = x[..., 0::2]
            x2 = x[..., 1::2]
            r1 = x1 * cos - x2 * sin
            r2 = x1 * sin + x2 * cos
            return jnp.stack([r1, r2], axis=-1).reshape(x.shape)
        b, s, _ = x.shape
        cos, sin = _rope_cos_sin(s, QK_ROPE)
        q = _rms_norm(x @ wq_a.T, q_norm_w) @ wq_b.T
        q = q.reshape(b, s, NH, QK_NOPE + QK_ROPE)
        q_nope, q_pe = (q[..., :QK_NOPE], q[..., QK_NOPE:])
        q_pe = _apply_rope(q_pe, cos[None, :, None, :], sin[None, :, None, :])
        kv = x @ wkv_a.T
        kv_c, k_pe = (kv[..., :KV_LORA], kv[..., KV_LORA:])
        k_pe = _apply_rope(k_pe, cos[None, :, :], sin[None, :, :])
        kv_up = _rms_norm(kv_c, kv_norm_w) @ wkv_b.T
        kv_up = kv_up.reshape(b, s, NH, QK_NOPE + V_DIM)
        k_nope, v = (kv_up[..., :QK_NOPE], kv_up[..., QK_NOPE:])
        scale = 1.0 / jnp.sqrt(jnp.float32(QK_NOPE + QK_ROPE))
        scores = (jnp.einsum('bshd,bthd->bhst', q_nope, k_nope) + jnp.einsum('bshd,btd->bhst', q_pe, k_pe)) * scale
        causal = jnp.tril(jnp.ones((s, s), bool))
        scores = jnp.where(causal[None, None], scores, jnp.finfo(scores.dtype).min)
        probs = jax.nn.softmax(scores, axis=-1)
        out = jnp.einsum('bhst,bthd->bshd', probs, v).reshape(b, s, NH * V_DIM)
        return out @ wo.T

    def _L0_ffn_ref(input, weight, bias):
        import jax, jax.numpy as jnp
        import numpy as np
        B, S, D_IN, D_OUT = (4, 256, 512, 512)
        out = jnp.einsum('bsi,oi->bso', input, weight)
        out = out + bias
        return out
    x = x + _L0_xattn_ref(_layernorm(x, axis=-1), ctx_4096, L0_xattn_Wq, L0_xattn_Wk, L0_xattn_Wv, L0_xattn_Wo)
    x = x + _L0_attn_ref(_layernorm(x, axis=-1), L0_attn_wq_a, L0_attn_q_norm_w, L0_attn_wq_b, L0_attn_wkv_a, L0_attn_kv_norm_w, L0_attn_wkv_b, L0_attn_wo)
    x = x + _L0_ffn_ref(_layernorm(x, axis=-1), L0_ffn_weight, L0_ffn_bias)
    return x

_drawn_inputs = setup_inputs


def setup_inputs(seed=0):
    import zlib

    import numpy as np

    out = dict(_drawn_inputs(seed))
    spreads = {'L0_attn_q_norm_w': (1.0, 0.6), 'L0_attn_kv_norm_w': (1.0, 0.6)}
    factors = {'L0_xattn_Wq': 6.398, 'L0_xattn_Wk': 6.382, 'L0_attn_wq_a': 8.0, 'L0_attn_wq_b': 8.0}
    for name, (base, spread) in spreads.items():
        noise = np.random.default_rng([zlib.crc32(name.encode()), seed]).standard_normal(out[name].shape)
        drawn = base * np.exp(spread * noise) if base else spread * noise
        out[name] = jnp.asarray(drawn.astype(out[name].dtype))
    for name, factor in factors.items():
        out[name] = (out[name] * factor).astype(out[name].dtype)
    return out
```

```python
from contextlib import ExitStack

import numpy as np

import concourse.bass as bass
from concourse import mybir

ALU = mybir.AluOpType
ACT = mybir.ActivationFunctionType
AX = mybir.AxisListType
F32 = mybir.dt.float32
F32R = mybir.dt.float32r
F16 = mybir.dt.float16

P = 128
B, S, D = 8, 32, 512
TOK = B * S
TT = TOK // P
KC = D // P
CTX = 512
H, KV, HD = 16, 4, 96
G = H // KV
KVD = KV * HD
KEYS = CTX + S
HALF = KEYS // 2
NK = KVD // P
NV = CTX // P
NU = NK + NV
XSCALE = 1.0 / float(np.sqrt(np.float32(HD)))
NH, NOPE, ROPE, VD = 32, 128, 64, 128
QL, KL = 192, 64
QB = QL - P
LAT = QL + KL + ROPE
MSCALE = 1.0 / float(np.sqrt(np.float32(NOPE + ROPE)))
LN_EPS, RMS_EPS = 1e-5, 1e-6
NHG = NH // 4

B_PROJ, B_S, B_PT, B_O = 0, 2, 4, 6


def blocks_of(j):
    out, r = [], 0
    while r < P:
        head, at = divmod(P * j + r, HD)
        n = min(HD - at, P - r)
        out.append((r, head, at, n))
        r += n
    return out


def build(nc, A, out):
    with ExitStack() as ctx:
        def sb(name, shape, dt=F32, scope=ctx):
            return scope.enter_context(nc.sbuf_tensor(name, shape, dt))

        def sem(name):
            return ctx.enter_context(nc.semaphore(name))

        def overlay(region, nbytes, *groups):
            made = []
            for group in groups:
                with ExitStack() as scope:
                    made.append([sb(n, s, d, scope) for n, s, d in group])
            sb(region, [P, nbytes // 4])
            return made

        ps = ctx.enter_context(nc.psum_tensor("ps", [P, 8, 512], F32))

        xs = sb("xs", [P, TT, D])
        xnT = sb("xnT", [P, KC, TOK])
        ident = sb("ident", [P, P])
        ropek = sb("ropek", [P, 2, 32])
        ropeq = sb("ropeq", [P, 2, 32])
        cap = sb("cap", [P, 32])
        qnw = sb("qnw", [P, QL])
        kvnw = sb("kvnw", [P, KL])
        bias = sb("bias", [P, D], F16)
        small = sb("small", [P, 96])

        (wkh, wkl, wvh, wvl), (wv2, pm) = overlay(
            "r_wkv", 24576,
            [("wkh", [P, KC, KVD], F32R), ("wkl", [P, KC, KVD], F32R),
             ("wvh", [P, KC, KVD], F32R), ("wvl", [P, KC, KVD], F32R)],
            [("wv2", [P, NH, VD], F32), ("pm", [P, 4, 512], F32)])
        (wq,), (wox,), (oT,) = overlay(
            "r_wq", 32768,
            [("wq", [P, KC, H * HD], F32)], [("wox", [HD, H, D], F32)], [("oT", [P, NH, TOK], F32)])
        (raw, hh0, hl0, hh1, hl1), (wqpa, wqpb, wa, qla, qlb), (ptm, oc) = overlay(
            "r_hid", 40960,
            [("raw", [P, KC, CTX], F32), ("hh0", [P, KC, CTX], F32R), ("hl0", [P, KC, CTX], F32R),
             ("hh1", [P, KC, CTX], F32R), ("hl1", [P, KC, CTX], F32R)],
            [("wqpa", [P, NH, P], F32), ("wqpb", [QB, NH, P], F32), ("wa", [P, KC, LAT], F32),
             ("qla", [P, TOK], F32), ("qlb", [QB, TOK], F32)],
            [("ptm", [P, TT, NHG, P], F32), ("oc", [P, 4, NH, S], F32)])
        hh, hl = (hh0, hh1), (hl0, hl1)
        (kt1, kt0, v0, v1), (xh, xl), (wqb, wkn), (qp,), (wo3, wf16, wf) = overlay(
            "r_kv", 33280,
            [("kt1", [HD, KV, KEYS], F32), ("kt0", [HD, KV, KEYS], F32),
             ("v0", [P, NV + 1, KVD], F32), ("v1", [P, NV + 1, KVD], F32)],
            [("xh", [P, KC, TOK], F32R), ("xl", [P, KC, TOK], F32R)],
            [("wqb", [P, NH, QL], F32), ("wkn", [P, NH, KL], F32)],
            [("qp", [P, B, NH, S], F32)],
            [("wo3", [P, 8, D], F32), ("wf16", [P, KC, D], F16), ("wf", [P, KC, D], F32)])
        kt, vv = (kt0, kt1), (v0, v1)
        (qT,), (wst,), (wo0,) = overlay(
            "r_qT", 16384, [("qT", [HD, H, TOK], F32)], [("wst", [P, 2, KC, KVD], F32)], [("wo0", [P, 8, D], F32)])
        (outT,), (qst,), (wo1,) = overlay(
            "r_out", 16384, [("outT", [HD, H, TOK], F32)], [("qst", [P, 12, TOK], F32)], [("wo1", [P, 8, D], F32)])
        (kst, qc0, qc1, klat, klst, vlst, pr, pt, pt4), (wo2, t2) = overlay(
            "r_misc", 25216,
            [("kst", [P, NK, CTX], F32), ("qc0", [HD, H, S], F32), ("qc1", [HD, H, S], F32),
             ("klat", [HD, KV, TOK], F32), ("klst", [P, NK, TOK], F32), ("vlst", [P, TT, KVD], F32),
             ("pr", [P, KEYS], F32), ("pt", [P, 512], F32), ("pt4", [S, P], F32)],
            [("wo2", [P, 8, D], F32), ("t2", [P, 2, 512], F32)])
        qc = (qc0, qc1)
        wo = (wo0, wo1, wo2, wo3)
        xn = sb("xn", [P, TT, D])
        kp = sb("kp", [P, TT, P])
        bd = sb("bd", [P, TT, 2, P])
        ql = sb("ql", [P, TT, QL])
        kpT = sb("kpT", [P, TOK])
        vlat = nc.dram_tensor("vlat_scratch", [TOK, KVD], F32, kind="Internal").ap()

        s_x, s_const, s_wkv, s_wq, s_wox = (sem(n) for n in ("s_x", "s_const", "s_wkv", "s_wq", "s_wox"))
        s_ctx = sem("s_ctx")
        s_hi, s_lo = sem("s_hi"), sem("s_lo")
        s_wsplit = sem("s_wsplit")
        s_v = sem("s_v")
        s_a = sem("s_a")
        s_g = sem("s_g")
        s_var, s_sd = sem("s_var"), sem("s_sd")
        s_xn = sem("s_xn")
        s_tp, s_xT = sem("s_tp"), sem("s_xT")
        s_xsp = sem("s_xsp")
        s_pm, s_pe = sem("s_pm"), sem("s_pe")
        s_qd = sem("s_qd")
        s_vl = sem("s_vl")
        s_ps = sem("s_ps")
        s_kev, s_vev = sem("s_kev"), sem("s_vev")
        s_kt = sem("s_kt")
        s_qc = sem("s_qc")
        s_s, s_nm, s_exp, s_pn, s_t, s_pt, s_pt4, s_o, s_oe = (
            sem(n) for n in ("s_s", "s_nm", "s_exp", "s_pn", "s_t", "s_pt", "s_pt4", "s_o", "s_oe"))
        s_y = sem("s_y")
        s_res = sem("s_res")
        s_wb = sem("s_wb")
        s_wc = sem("s_wc")
        s_cm, s_ce = sem("s_cm"), sem("s_ce")
        s_lat, s_sq, s_qk = sem("s_lat"), sem("s_sq"), sem("s_qk")
        s_lt, s_lte = sem("s_lt"), sem("s_lte")
        s_bd = sem("s_bd")
        s_qm, s_qa, s_qv, s_qr = sem("s_qm"), sem("s_qa"), sem("s_qv"), sem("s_qr")
        s_ms, s_mm, s_me, s_mp = sem("s_ms"), sem("s_mm"), sem("s_me"), sem("s_mp")
        s_mt, s_mte = sem("s_mt"), sem("s_mte")
        s_pv, s_pve = sem("s_pv"), sem("s_pve")
        s_up, s_upa, s_upv = sem("s_up"), sem("s_upa"), sem("s_upv")
        s_wo = [sem(f"s_wo{i}") for i in range(4)]
        s_wv2, s_wf, s_wfc = sem("s_wv2"), sem("s_wf"), sem("s_wfc")
        s_out = sem("s_out")

        mv = small[:, 0:4].rearrange("p (t c) -> p t c", t=TT)
        bns = small[:, 4:16].rearrange("p (t c) -> p t c", t=TT)
        va, sd, rr, nt = (small[:, 16 + 4 * i:20 + 4 * i] for i in range(4))
        mx, nm, rs, ri = (small[:, 32 + 4 * i:36 + 4 * i] for i in range(4))
        ssq = small[:, 48:52]
        mmx = small[:, 52:68]
        msum = small[:, 68:84]

        block = ctx.enter_context(nc.Block())

        @block.sync
        def _(sp):
            sp.dma_start(raw[:], A["ctxT"][0]).then_inc(s_ctx, 16)
            sp.dma_start(wst[:, 0], A["wkT"]).then_inc(s_wkv, 16)
            sp.dma_start(xs[:], A["x"].rearrange("(t p) d -> p t d", p=P)).then_inc(s_x, 16)
            sp.dma_start(wst[:, 1], A["wvT"]).then_inc(s_wkv, 16)
            sp.dma_start(wq[:], A["wqT"]).then_inc(s_wq, 16)
            for b in range(1, 3):
                sp.wait_ge(s_lo, KC * b)
                sp.dma_start(raw[:], A["ctxT"][b]).then_inc(s_ctx, 16)

            def relay(b, par):
                for j in range(NK):
                    sp.wait_ge(s_kev, NK * b + j + 1)
                    for r, g, at, n in blocks_of(j):
                        sp.dma_start(kt[par][at:at + n, g, 0:CTX], kst[r:r + n, j, :]).then_inc(s_kt, 16)
                sp.dma_start(kt[par][:, :, CTX:KEYS], klat[:, :, bass.ds(b * S, S)]).then_inc(s_kt, 16)
                sp.dma_start(vv[par][0:S, NV, :], vlat[bass.ds(b * S, S), :]).then_inc(s_kt, 16)

            for m in range(NK):
                sp.wait_ge(s_pe, m + 1)
                for r, g, at, n in blocks_of(m):
                    sp.dma_start(klat[at:at + n, g, :], klst[r:r + n, m, :]).then_inc(s_qd, 16)
            for t in range(TT):
                sp.wait_ge(s_pe, NK + t + 1)
                sp.dma_start(vlat[P * t:P * t + P, :], vlst[:, t, :]).then_inc(s_vl, 16)
            for m in range(H * HD // P):
                sp.wait_ge(s_pe, NK + TT + m + 1)
                for r, h, at, n in blocks_of(m):
                    sp.dma_start(qT[at:at + n, h, :], qst[r:r + n, m, :]).then_inc(s_qd, 16)
            sp.wait_ge(s_qd, 16 * (6 + 24))
            sp.wait_ge(s_vl, 16 * TT)
            sp.dma_start(wox[:], A["woxT"]).then_inc(s_wox, 16)
            relay(0, 0)

            def step(b, par, more, load):
                sp.wait_ge(s_s, KV * b) if not isinstance(b, int) or b > 0 else None
                if more:
                    if not isinstance(b, int) or b > 0:
                        sp.wait_ge(s_o, KV * b)
                    relay(b + 1, 1 - par)
                if load:
                    sp.wait_ge(s_lo, KC * (b + 3))
                    sp.dma_start(raw[:], A["ctxT"][b + 3]).then_inc(s_ctx, 16)

            for b in range(B):
                step(b, b % 2, b + 1 < B, b + 3 < B)

            sp.wait_ge(s_ps, NU * B)
            sp.dma_start(wqpa[:, :, KL:P], A["wqra"]).then_inc(s_wb, 16)
            sp.dma_start(wqpb[:, :, KL:P], A["wqrb"]).then_inc(s_wb, 16)
            sp.dma_start(wa[:], A["waT"]).then_inc(s_wb, 16)
            sp.wait_ge(s_o, KV * B)
            sp.dma_start(wqb[:], A["wqbn"]).then_inc(s_wc, 16)
            sp.dma_start(wkn[:], A["wkn"]).then_inc(s_wc, 16)
            sp.dma_start(wv2[0:KL], A["wvb"]).then_inc(s_wv2, 16)
            sp.dma_start(wv2[KL:P], A["wvb"]).then_inc(s_wv2, 16)
            sp.dma_start(wo0[:], A["wob"][:, 0:8, :]).then_inc(s_wo[0], 16)
            sp.dma_start(wo2[:], A["wob"][:, 16:24, :]).then_inc(s_wo[2], 16)
            sp.wait_ge(s_y, 2)
            sp.dma_start(wo1[:], A["wob"][:, 8:16, :]).then_inc(s_wo[1], 16)
            sp.wait_ge(s_ms, 4)
            sp.dma_start(wo3[:], A["wob"][:, 24:32, :]).then_inc(s_wo[3], 16)
            sp.dma_start(wf16[:], A["wfT"]).then_inc(s_wf, 16)
            for t in range(TT):
                sp.wait_ge(s_res, 2 * TT + t + 1)
                sp.dma_start(out[P * t:P * t + P, :], xs[:, t, :]).then_inc(s_out, 16)
            sp.wait_ge(s_out, 16 * TT)

        @block.gpsimd
        def _(pool):
            pool.dma_start(ident[:], A["ident"]).then_inc(s_const, 16)
            pool.dma_start(ropek[:], A["ropek"]).then_inc(s_const, 16)
            pool.dma_start(ropeq[:], A["ropeq"]).then_inc(s_const, 16)
            pool.dma_start(cap[:], A["cap"]).then_inc(s_const, 16)
            pool.dma_start(qnw[:], A["qnw"].partition_broadcast(P)).then_inc(s_const, 16)
            pool.dma_start(kvnw[:], A["kvnw"].partition_broadcast(P)).then_inc(s_const, 16)
            pool.dma_start(bias[:], A["bias"].partition_broadcast(P)).then_inc(s_const, 16)
            pool.memset(bd[:], 0.0).then_inc(s_g, 1)

            def split(b, par, k):
                pool.wait_ge(s_hi, KC * b + k + 1)
                pool.tensor_tensor(hl[par][:, k, :], raw[:, k, :], hh[par][:, k, :], ALU.subtract).then_inc(s_lo, 1)

            def queries(b, par):
                pool.tensor_copy(qc[par][:], qT[:, :, bass.ds(b * S, S)]).then_inc(s_qc, 1)

            for k in range(KC):
                split(0, 0, k)
            for k in range(KC):
                split(1, 1, k)
            pool.wait_ge(s_qd, 16 * (6 + 24))
            queries(0, 0)

            def step(b, par, more, ahead):
                if more:
                    if not isinstance(b, int) or b > 0:
                        pool.wait_ge(s_s, KV * b)
                    queries(b + 1, 1 - par)
                if ahead:
                    for k in range(KC):
                        split(b + 2, par, k)

            for b in range(B):
                step(b, b % 2, b + 1 < B, b + 2 < B)

            for n in range(NH // 2):
                pool.wait_ge(s_qv, n + 1)
                rows = qp[KL:P, :, 2 * n:2 * n + 2, :]
                part = t2[KL:P, n % 2, :].rearrange("p (h b s) -> p b h s", h=2, s=S)
                pool.tensor_tensor(rows, rows, part, ALU.add).then_inc(s_qr, 1)

        @block.scalar
        def _(act):
            def root(n, lo, hi):
                act.wait_ge(s_var, n)
                act.activation(sd[:, lo:hi], va[:, lo:hi], ACT.Sqrt).then_inc(s_sd, 1)

            def turn_out(n):
                for t in range(TT):
                    act.wait_ge(s_tp, TT * n + t + 1)
                    act.copy(xnT[:, :, P * t:P * t + P],
                             ps[:, B_S + t, :].rearrange("p (k c) -> p k c", k=KC)).then_inc(s_xT, 1)

            def v_out(b, par, i):
                n = NU * b + NK + i
                act.wait_ge(s_ps, n + 1)
                bank = B_PROJ + (par + NK + i) % 2
                act.copy(vv[par][:, i, :], ps[:, bank, 0:KVD]).then_inc(s_vev, 1)

            root(1, 0, TT)
            for i in range(NV):
                v_out(0, 0, i)
            turn_out(0)
            act.wait_ge(s_xT, TT)
            act.copy(xh[:], xnT[:]).then_inc(s_xsp, 1)
            for m in range(NK + TT + H * HD // P):
                act.wait_ge(s_pm, m + 1)
                bank = ps[:, B_PT + m % 4, :]
                if m < NK:
                    dst, src = klst[:, m, :], bank[:, 0:TOK]
                elif m < NK + TT:
                    dst, src = vlst[:, m - NK, :], bank[:, 0:KVD]
                else:
                    dst, src = qst[:, m - NK - TT, :], bank[:, 0:TOK]
                act.copy(dst, src).then_inc(s_pe, 1)

            def step(b, par, more):
                for g in range(KV):
                    n = KV * b + g
                    act.wait_ge(s_nm, n + 1)
                    if not isinstance(b, int) or n > 0:
                        act.wait_ge(s_t, n)
                    act.activation(pr[:].rearrange("p (a k) -> p a k", a=2), ps[:, B_S:B_S + 2, 0:HALF], ACT.Exp,
                                   bias=nm[:, g:g + 1], scale=XSCALE, accum_out=rs[:, g:g + 1]).then_inc(s_exp, 1)
                    if more and g >= 2:
                        v_out(b + 1, 1 - par, 2 * g - NK)
                    act.wait_ge(s_t, n + 1)
                    if not isinstance(b, int) or n > 0:
                        act.wait_ge(s_o, n)
                    act.copy(pt[:], ps[:, B_PT, :]).then_inc(s_pt, 1)
                    if more and g in (1, 2):
                        v_out(b + 1, 1 - par, 2 * g + 1 - NK)

            for b in range(B):
                step(b, b % 2, b + 1 < B)

            root(2, 0, TT)
            turn_out(1)
            for t in range(TT):
                act.wait_ge(s_lat, t + 1)
                if t == 0:
                    act.wait_ge(s_xn, 2 * TT)
                    act.wait_ge(s_tp, 2 * TT)
                act.activation(xn[:, t, 0:QL], ps[:, B_PT + t, 0:QL], ACT.Square,
                               accum_out=ssq[:, t:t + 1]).then_inc(s_sq, 1)
                act.activation(xn[:, t, QL:QL + KL], ps[:, B_PT + t, QL:QL + KL], ACT.Square,
                               accum_out=ssq[:, TT + t:TT + t + 1]).then_inc(s_sq, 1)
            root(3, 0, 2 * TT)
            act.wait_ge(s_lt, 1)
            act.copy(qla[:], ps[:, B_O, 0:TOK]).then_inc(s_lte, 1)
            act.copy(qlb[:], ps[0:QB, B_O, TOK:2 * TOK]).then_inc(s_lte, 1)
            act.copy(kpT[:], ps[:, B_O + 1, 0:TOK]).then_inc(s_lte, 1)
            for n in range(NH // 2):
                act.wait_ge(s_qm, n + 1)
                act.copy(qp[0:KL, :, 2 * n:2 * n + 2, :],
                         ps[0:KL, n % 2, :].rearrange("p (h b s) -> p b h s", h=2, s=S)).then_inc(s_qa, 1)
            for w in range(4):
                act.wait_ge(s_mm, w + 1)
                act.activation(pm[:, w, :], pm[:, w, :], ACT.Exp, scale=MSCALE).then_inc(s_me, 1)
            for w in range(4):
                act.wait_ge(s_mt, w + 1)
                act.copy(ptm[:, :, 2 * w:2 * w + 2, :],
                         ps[:, B_O + w % 2, :].rearrange("p (t g c) -> p t g c", t=TT, g=2)).then_inc(s_mte, 1)
            for n in range(8):
                act.wait_ge(s_pv, n + 1)
                act.copy(oc[:, n // 2, 16 * (n % 2):16 * (n % 2) + 16, :],
                         ps[:, n % 2, :].rearrange("p (h s) -> p h s", s=S)).then_inc(s_pve, 1)
            for n in range(NH // 4):
                act.wait_ge(s_up, n + 1)
                act.copy(oT[:, 4 * n:4 * n + 4, :].rearrange("p h (k v s) -> p h k v s", v=2, s=S)[:, :, :, 0, :],
                         ps[:, B_S + 2 * (n % 2), :].rearrange("p (h k s) -> p h k s", h=4, s=S)).then_inc(s_upa, 1)
            root(4, 0, TT)
            turn_out(2)

        @block.vector
        def _(dve):
            chain = [0]

            def link(ins):
                chain[0] += 1
                ins.then_inc(s_v, 1)
                dve.wait_ge(s_v, chain[0])

            def inverse_root(n, lo, hi):
                dve.wait_ge(s_sd, n)
                link(dve.reciprocal(rr[:, lo:hi], sd[:, lo:hi]))
                link(dve.tensor_tensor(nt[:, lo:hi], rr[:, lo:hi], rr[:, lo:hi], ALU.mult))
                link(dve.tensor_tensor(nt[:, lo:hi], nt[:, lo:hi], va[:, lo:hi], ALU.mult))
                link(dve.tensor_scalar(nt[:, lo:hi], nt[:, lo:hi], -0.5, 1.5, ALU.mult, ALU.add))
                link(dve.tensor_tensor(rr[:, lo:hi], rr[:, lo:hi], nt[:, lo:hi], ALU.mult))

            def layernorm(n):
                for t in range(TT):
                    link(dve.bn_stats(bns[:, t, :], xs[:, t, :]))
                    link(dve.bn_aggr(mv[:, t, :], bns[:, t, :]))
                dve.tensor_scalar(va[:, 0:TT], mv[:, :, 1], LN_EPS, None, ALU.add).then_inc(s_var, 1)
                inverse_root(n, 0, TT)
                for t in range(TT):
                    dve.tensor_scalar(xn[:, t, :], xs[:, t, :], mv[:, t, 0:1], rr[:, t:t + 1],
                                      ALU.subtract, ALU.mult).then_inc(s_xn, 1)

            def high(b, par, k):
                dve.tensor_copy(hh[par][:, k, :], raw[:, k, :]).then_inc(s_hi, 1)

            def k_out(b, par, j):
                dve.wait_ge(s_ps, NU * b + j + 1)
                dve.tensor_copy(kst[:, j, :], ps[:, B_PROJ + (par + j) % 2, :]).then_inc(s_kev, 1)

            dve.wait_ge(s_ctx, 16)
            for k in range(KC):
                high(0, 0, k)
            dve.wait_ge(s_wkv, 32)
            link(dve.tensor_copy(wkh[:], wst[:, 0]))
            dve.tensor_tensor(wkl[:], wst[:, 0], wkh[:], ALU.subtract).then_inc(s_wsplit, 1)
            dve.wait_ge(s_x, 16)
            layernorm(1)
            link(dve.tensor_copy(wvh[:], wst[:, 1]))
            dve.tensor_tensor(wvl[:], wst[:, 1], wvh[:], ALU.subtract).then_inc(s_wsplit, 1)
            for j in range(NK):
                k_out(0, 0, j)
            dve.wait_ge(s_ctx, 32)
            for k in range(KC):
                high(1, 1, k)
            dve.wait_ge(s_xsp, 1)
            dve.tensor_tensor(xl[:], xnT[:], xh[:], ALU.subtract).then_inc(s_xsp, 1)

            def o_out(b, g):
                dve.wait_ge(s_o, KV * b + g + 1)
                dve.tensor_copy(outT[:, G * g:G * g + G, bass.ds(b * S, S)],
                                ps[0:HD, B_O + g % 2, 0:P].rearrange("p (h s) -> p h s", h=G)).then_inc(s_oe, 1)

            def step(b, par, more, ahead):
                for g in range(KV):
                    n = KV * b + g
                    dve.wait_ge(s_s, n + 1)
                    link(dve.tensor_reduce(mx[:, g:g + 1], ps[:, B_S:B_S + 2, 0:HALF], AX.XY, ALU.max))
                    dve.tensor_scalar(nm[:, g:g + 1], mx[:, g:g + 1], -XSCALE, None, ALU.mult).then_inc(s_nm, 1)
                    if g > 0:
                        o_out(b, g - 1)
                    elif not isinstance(b, int) or b > 0:
                        o_out(b - 1, KV - 1)
                    if more and 2 * g < NK:
                        if g == 0:
                            dve.wait_ge(s_kt, P * (b + 1))
                        k_out(b + 1, 1 - par, 2 * g)
                    dve.wait_ge(s_exp, n + 1)
                    link(dve.reciprocal(ri[:, g:g + 1], rs[:, g:g + 1]))
                    dve.tensor_scalar(pr[:], pr[:], ri[:, g:g + 1], None, ALU.mult).then_inc(s_pn, 1)
                    if ahead:
                        if g == 0:
                            dve.wait_ge(s_ctx, 16 * (b + 3))
                            dve.wait_ge(s_ps, NU * (b + 1))
                        high(b + 2, par, g)
                    dve.wait_ge(s_t, n + 1)
                    dve.tensor_copy(pt4[:], ps[0:S, B_PT + 1, 0:P]).then_inc(s_pt4, 1)
                    if more and 2 * g + 1 < NK:
                        k_out(b + 1, 1 - par, 2 * g + 1)

            for b in range(B):
                step(b, b % 2, b + 1 < B, b + 2 < B)
            o_out(B - 1, KV - 1)

            for t in range(TT):
                dve.wait_ge(s_y, t + 1)
                dve.tensor_tensor(xs[:, t, :], xs[:, t, :], ps[:, B_PROJ + t, :], ALU.add).then_inc(s_res, 1)
            dve.wait_ge(s_res, TT)
            layernorm(2)
            for m in range(4):
                dve.wait_ge(s_cm, m + 1)
                dve.tensor_copy(wqpa[:, 8 * m:8 * m + 8, 0:KL],
                                ps[:, B_PT + 2 * (m % 2), :].rearrange("p (h c) -> p h c", h=8)).then_inc(s_ce, 1)
                dve.tensor_copy(wqpb[:, 8 * m:8 * m + 8, 0:KL],
                                ps[0:QB, B_PT + 2 * (m % 2) + 1, :].rearrange("p (h c) -> p h c", h=8)
                                ).then_inc(s_ce, 1)
            dve.wait_ge(s_sq, 2 * TT)
            link(dve.tensor_scalar(va[:, 0:TT], ssq[:, 0:TT], 1.0 / QL, RMS_EPS, ALU.mult, ALU.add))
            dve.tensor_scalar(va[:, TT:2 * TT], ssq[:, TT:2 * TT], 1.0 / KL, RMS_EPS,
                              ALU.mult, ALU.add).then_inc(s_var, 1)
            inverse_root(3, 0, 2 * TT)
            for t in range(TT):
                lat = ps[:, B_PT + t, :]
                dve.scalar_tensor_tensor(out=ql[:, t, :], in0=lat[:, 0:QL], scalar=rr[:, t:t + 1], in1=qnw[:],
                                         op0=ALU.mult, op1=ALU.mult).then_inc(s_qk, 1)
                link(dve.scalar_tensor_tensor(out=kp[:, t, 0:KL], in0=lat[:, QL:QL + KL],
                                              scalar=rr[:, TT + t:TT + t + 1], in1=kvnw[:],
                                              op0=ALU.mult, op1=ALU.mult))
            x1 = ps[:, B_PT:B_PT + TT, QL + KL:QL + KL + 32]
            x2 = ps[:, B_PT:B_PT + TT, QL + KL + 32:LAT]
            cos, sin = (ropek[:, i:i + 1, :].to_broadcast([P, TT, 32]) for i in range(2))
            rot = xn[:, 0, 256:512].rearrange("p (a t c) -> p a t c", a=4, t=TT)
            for i, (a, w) in enumerate(((x1, cos), (x2, sin), (x1, sin), (x2, cos))):
                link(dve.tensor_tensor(rot[:, i], a, w, ALU.mult))
            dve.tensor_tensor(kp[:, :, KL:KL + 32], rot[:, 0], rot[:, 1], ALU.subtract).then_inc(s_qk, 1)
            dve.tensor_tensor(kp[:, :, KL + 32:P], rot[:, 2], rot[:, 3], ALU.add).then_inc(s_qk, 1)
            dve.wait_ge(s_g, 1)
            for u in range(4):
                r = slice(S * u, S * u + S)
                dve.tensor_copy(bd[r, :, u // 2, KL * (u % 2):KL * (u % 2) + KL], kp[r, :, 0:KL]).then_inc(s_bd, 1)
            for n in range(NH // 2):
                dve.wait_ge(s_qm, n + 1)
                if n >= 2:
                    dve.wait_ge(s_qr, n - 1)
                q = ps[:, n % 2, :].rearrange("p (a s) -> p a s", s=S)
                qb = ps[:, n % 2, :].rearrange("p (h b s) -> p b h s", h=2, s=S)
                tt = t2[:, n % 2, :].rearrange("p (a s) -> p a s", s=S)
                dst = qp[:, :, 2 * n:2 * n + 2, :]

                def tab(lo, hi):
                    return ropeq[lo:hi, 1:2, :].to_broadcast([hi - lo, 2 * B, S])

                cosb = ropeq[KL:P, 0:1, :].unsqueeze(1).to_broadcast([P - KL, B, 2, S])
                dve.tensor_tensor(dst[KL:P], qb[KL:P], cosb, ALU.mult).then_inc(s_v, 1)
                dve.tensor_tensor(tt[KL:KL + 32], q[KL + 32:P], tab(KL + 32, P), ALU.mult).then_inc(s_v, 1)
                chain[0] += 2
                dve.tensor_tensor(tt[KL + 32:P], q[KL:KL + 32], tab(KL, KL + 32), ALU.mult).then_inc(s_qv, 1)
            capb = cap[:].unsqueeze(1).to_broadcast([P, 16, 32])
            for w in range(4):
                sc = pm[:, w, :].rearrange("p (a t) -> p a t", a=16)
                dve.wait_ge(s_ms, w + 1)
                link(dve.tensor_tensor(sc, ps[:, B_S + w, :].rearrange("p (a t) -> p a t", a=16), capb, ALU.min))
                link(dve.tensor_reduce(mmx[:], sc, AX.X, ALU.max))
                dve.tensor_tensor(sc, sc, mmx[:].unsqueeze(2).to_broadcast([P, 16, 32]), ALU.subtract
                                  ).then_inc(s_mm, 1)
                dve.wait_ge(s_me, w + 1)
                link(dve.tensor_reduce(msum[:], sc, AX.X, ALU.add))
                link(dve.reciprocal(msum[:], msum[:]))
                dve.tensor_tensor(sc, sc, msum[:].unsqueeze(2).to_broadcast([P, 16, 32]), ALU.mult
                                  ).then_inc(s_mp, 1)
            for n in range(NH // 4):
                dve.wait_ge(s_up, n + 1)
                dve.tensor_copy(
                    oT[:, 4 * n:4 * n + 4, :].rearrange("p h (k v s) -> p h k v s", v=2, s=S)[:, :, :, 1, :],
                    ps[:, B_S + 2 * (n % 2) + 1, :].rearrange("p (h k s) -> p h k s", h=4, s=S)).then_inc(s_upv, 1)
            dve.wait_ge(s_wf, 16)
            dve.tensor_copy(wf[:], wf16[:]).then_inc(s_wfc, 1)
            for t in range(TT):
                dve.wait_ge(s_y, TT + t + 1)
                dve.tensor_tensor(xs[:, t, :], xs[:, t, :], ps[:, B_O + t, :], ALU.add).then_inc(s_res, 1)
            dve.wait_ge(s_res, 2 * TT)
            layernorm(4)
            for t in range(TT):
                link(dve.tensor_tensor(xs[:, t, :], xs[:, t, :], bias[:], ALU.add))
            for t in range(TT):
                dve.wait_ge(s_y, 2 * TT + t + 1)
                dve.tensor_tensor(xs[:, t, :], xs[:, t, :], ps[:, B_PROJ + t, :], ALU.add).then_inc(s_res, 1)

        @block.tensor
        def _(pe):
            def three(bank, wide, lo_hi, xs_, k, first, last):
                (wh, wl), (mh, ml) = lo_hi, xs_
                for i, (w, m) in enumerate(((wh, mh), (wl, mh), (wh, ml))):
                    mm = pe.matmul(wide, w, m, start=first and i == 0, stop=last and i == 2)
                return mm

            def k_unit(b, par, j):
                bank = B_PROJ + (par + j) % 2
                c = slice(P * j, P * j + P)
                for k in range(KC):
                    mm = three(bank, ps[:, bank, :], (wkh[:, k, c], wkl[:, k, c]),
                               (hh[par][:, k, :], hl[par][:, k, :]), k, k == 0, k == KC - 1)
                mm.then_inc(s_ps, 1)

            def v_unit(b, par, i):
                bank = B_PROJ + (par + NK + i) % 2
                c = slice(P * i, P * i + P)
                for k in range(KC):
                    mm = three(bank, ps[:, bank, 0:KVD], (hh[par][:, k, c], hl[par][:, k, c]),
                               (wvh[:, k, :], wvl[:, k, :]), k, k == 0, k == KC - 1)
                mm.then_inc(s_ps, 1)

            def unit(b, par, u):
                if u == 0:
                    pe.wait_ge(s_lo, KC * (b + 1))
                if u < 2:
                    if not isinstance(b, int) or b > 0:
                        pe.wait_ge(s_vev, NV * (b - 1) + 3 + u)
                elif u < NK + 2:
                    pe.wait_ge(s_kev, NK * b + u - 1)
                else:
                    pe.wait_ge(s_vev, NV * b + u - NK - 1)
                k_unit(b, par, u) if u < NK else v_unit(b, par, u - NK)

            def turn(n):
                for t in range(TT):
                    pe.wait_ge(s_xn, TT * n + t + 1)
                    for k in range(KC):
                        tr = pe.transpose(ps[:, B_S + t, P * k:P * k + P], xn[:, t, P * k:P * k + P], ident[:])
                    tr.then_inc(s_tp, 1)

            pe.wait_ge(s_wsplit, 1)
            for u in range(NU):
                if u == NK:
                    pe.wait_ge(s_wsplit, 2)
                unit(0, 0, u)
            pe.wait_ge(s_const, 16 * 7)
            turn(0)
            pe.wait_ge(s_xsp, 2)
            for m in range(NK + TT + H * HD // P):
                if m >= 4:
                    pe.wait_ge(s_pe, m - 3)
                bank = B_PT + m % 4
                if m == NK + TT:
                    pe.wait_ge(s_wq, 16)
                for k in range(KC):
                    if m < NK:
                        c = slice(P * m, P * m + P)
                        mm = three(bank, ps[:, bank, 0:TOK], (wkh[:, k, c], wkl[:, k, c]),
                                   (xh[:, k, :], xl[:, k, :]), k, k == 0, k == KC - 1)
                    elif m < NK + TT:
                        c = slice(P * (m - NK), P * (m - NK) + P)
                        mm = three(bank, ps[:, bank, 0:KVD], (xh[:, k, c], xl[:, k, c]),
                                   (wvh[:, k, :], wvl[:, k, :]), k, k == 0, k == KC - 1)
                    else:
                        c = slice(P * (m - NK - TT), P * (m - NK - TT) + P)
                        mm = pe.matmul(ps[:, bank, 0:TOK], wq[:, k, c], xnT[:, k, :], start=(k == 0), stop=(k == KC - 1))
                mm.then_inc(s_pm, 1)

            def scores(b, par, g):
                if g == 0:
                    pe.wait_ge(s_qc, b + 1)
                    pe.wait_ge(s_kt, P * (b + 1))
                for a in range(2):
                    mm = pe.matmul(ps[:, B_S + a, 0:HALF], qc[par][:, G * g:G * g + G, :].rearrange("p h s -> p (h s)"),
                                   kt[par][:, g, HALF * a:HALF * a + HALF], start=True, stop=True)
                mm.then_inc(s_s, 1)

            def step(b, par, more):
                for g in range(KV):
                    n = KV * b + g
                    if more:
                        unit(b + 1, 1 - par, 2 * g)
                    pe.wait_ge(s_pn, n + 1)
                    if not isinstance(b, int) or n > 0:
                        pe.wait_ge(s_pt, n)
                        pe.wait_ge(s_pt4, n)
                    for j in range(NV):
                        pe.transpose(ps[:, B_PT, P * j:P * j + P], pr[:, P * j:P * j + P], ident[:])
                    pe.transpose(ps[0:S, B_PT + 1, 0:P], pr[:, CTX:KEYS], ident[:]).then_inc(s_t, 1)
                    if more and 2 * g + 1 < NU:
                        unit(b + 1, 1 - par, 2 * g + 1)
                    if g + 1 < KV:
                        scores(b, par, g + 1)
                    elif more:
                        scores(b + 1, 1 - par, 0)
                    pe.wait_ge(s_pt, n + 1)
                    pe.wait_ge(s_pt4, n + 1)
                    if g == 0:
                        pe.wait_ge(s_vev, NV * (b + 1))
                    if not isinstance(b, int) or n > 1:
                        pe.wait_ge(s_oe, n - 1)
                    o = ps[0:HD, B_O + g % 2, 0:P]
                    for j in range(NV):
                        pe.matmul(o, vv[par][:, j, HD * g:HD * g + HD], pt[:, P * j:P * j + P], start=(j == 0), stop=False)
                    pe.matmul(o, vv[par][0:S, NV, HD * g:HD * g + HD], pt4[:], start=False, stop=True).then_inc(s_o, 1)

            scores(0, 0, 0)
            for b in range(B):
                step(b, b % 2, b + 1 < B)

            pe.wait_ge(s_wox, 16)
            pe.wait_ge(s_oe, KV * B)
            for t in range(TT):
                for h in range(H):
                    mm = pe.matmul(ps[:, B_PROJ + t, :], outT[:, h, P * t:P * t + P], wox[:, h, :],
                                   start=(h == 0), stop=(h == H - 1))
                mm.then_inc(s_y, 1)

            pe.wait_ge(s_wc, 32)
            for m in range(4):
                if m >= 2:
                    pe.wait_ge(s_ce, 2 * (m - 1))
                for i in range(8):
                    h = 8 * m + i
                    bank = B_PT + 2 * (m % 2)
                    pe.matmul(ps[:, bank, KL * i:KL * i + KL], wqb[:, h, 0:P], wkn[:, h, :], start=True, stop=True)
                    mm = pe.matmul(ps[0:QB, bank + 1, KL * i:KL * i + KL], wqb[:, h, P:QL], wkn[:, h, :],
                                   start=True, stop=True)
                mm.then_inc(s_cm, 1)
            turn(1)
            pe.wait_ge(s_wb, 48)
            pe.wait_ge(s_ce, 8)
            pe.wait_ge(s_xT, 2 * TT)
            for t in range(TT):
                for k in range(KC):
                    mm = pe.matmul(ps[:, B_PT + t, 0:LAT], xnT[:, k, P * t:P * t + P], wa[:, k, :],
                                   start=(k == 0), stop=(k == KC - 1))
                mm.then_inc(s_lat, 1)
            pe.wait_ge(s_qk, TT + 2)
            for t in range(TT):
                pe.transpose(ps[:, B_O, P * t:P * t + P], ql[:, t, 0:P], ident[:])
                pe.transpose(ps[0:QB, B_O, TOK + P * t:TOK + P * t + P], ql[:, t, P:QL], ident[:])
                tr = pe.transpose(ps[:, B_O + 1, P * t:P * t + P], kp[:, t, :], ident[:])
            tr.then_inc(s_lt, 1)
            pe.wait_ge(s_lte, 3)
            for n in range(NH // 2):
                if n >= 2:
                    pe.wait_ge(s_qa, n - 1)
                    pe.wait_ge(s_qv, n - 1)
                for i in range(2):
                    h = 2 * n + i
                    o = ps[:, n % 2, TOK * i:TOK * i + TOK]
                    pe.matmul(o, wqpa[:, h, :], qla[:], start=True, stop=False)
                    mm = pe.matmul(o, wqpb[:, h, :], qlb[:], start=False, stop=True)
                mm.then_inc(s_qm, 1)
            for w in range(4):
                pe.wait_ge(s_qa, 4 * w + 4)
                pe.wait_ge(s_qr, 4 * w + 4)
                if w == 2:
                    pe.wait_ge(s_qk, TT + 2)
                for i in range(2):
                    for b in range(B):
                        g = 2 * w + i
                        mm = pe.matmul(ps[:, B_S + w, S * (B * i + b):S * (B * i + b) + S],
                                       qp[:, b, 4 * g:4 * g + 4, :].rearrange("p h s -> p (h s)"), kpT[:, S * b:S * b + S],
                                       start=True, stop=True)
                mm.then_inc(s_ms, 1)
            for w in range(4):
                pe.wait_ge(s_mp, w + 1)
                if w >= 2:
                    pe.wait_ge(s_mte, w - 1)
                for t in range(TT):
                    for i in range(2):
                        at = B * S * i + P * t
                        tr = pe.transpose(ps[:, B_O + w % 2, P * (2 * t + i):P * (2 * t + i) + P],
                                          pm[:, w, at:at + P], ident[:])
                tr.then_inc(s_mt, 1)
            pe.wait_ge(s_mte, 4)
            pe.wait_ge(s_bd, 4)
            for n in range(8):
                if n >= 2:
                    pe.wait_ge(s_pve, n - 1)
                tq, half = n // 2, n % 2
                pe.matmul(ps[:, n % 2, :], bd[:, tq // 2, tq % 2, :], ptm[:, tq // 2, 4 * half:4 * half + 4, :],
                          start=True, stop=True).then_inc(s_pv, 1)
            pe.wait_ge(s_pve, 8)
            pe.wait_ge(s_wv2, 32)

            def up(n):
                if n >= 2:
                    pe.wait_ge(s_upa, n - 1)
                    pe.wait_ge(s_upv, n - 1)
                for v in range(2):
                    for i in range(4):
                        mm = pe.matmul(ps[:, B_S + 2 * (n % 2) + v, P * i:P * i + P],
                                       wv2[KL * v:KL * v + KL, 4 * n + i, :], oc[KL * v:KL * v + KL, :, 4 * n + i, :],
                                       start=True, stop=True)
                mm.then_inc(s_up, 1)

            up(0)
            for n in range(NH // 4):
                if n + 1 < NH // 4:
                    up(n + 1)
                pe.wait_ge(s_upa, n + 1)
                pe.wait_ge(s_upv, n + 1)
                if n % 2 == 0:
                    pe.wait_ge(s_wo[n // 2], 16)
                for h in range(4 * n, 4 * n + 4):
                    for t in range(TT):
                        mm = pe.matmul(ps[:, B_O + t, :], oT[:, h, P * t:P * t + P], wo[h // 8][:, h % 8, :],
                                       start=(h == 0), stop=(h == NH - 1))
                        if h == NH - 1:
                            mm.then_inc(s_y, 1)
            turn(2)
            pe.wait_ge(s_wfc, 1)
            pe.wait_ge(s_xT, 3 * TT)
            for t in range(TT):
                for k in range(KC):
                    mm = pe.matmul(ps[:, B_PROJ + t, :], xnT[:, k, P * t:P * t + P], wf[:, k, :],
                                   start=(k == 0), stop=(k == KC - 1))
                mm.then_inc(s_y, 1)


def lay_out(a):
    f = {k: np.ascontiguousarray(v) for k, v in a.items()}

    def chunks(w):
        return w.T.reshape(KC, P, w.shape[0]).transpose(1, 0, 2)

    turn = np.concatenate([np.arange(0, ROPE, 2), np.arange(1, ROPE, 2)])
    kva = f["L0_attn_wkv_a"]
    wqb = f["L0_attn_wq_b"].reshape(NH, NOPE + ROPE, QL)
    wkvb = f["L0_attn_wkv_b"].reshape(NH, NOPE + VD, KL)
    wqr = wqb[:, NOPE:, :][:, turn, :].transpose(2, 0, 1)
    freq = (1.0 / 10000.0 ** (np.arange(0, ROPE, 2, dtype=np.float32) / np.float32(ROPE))).astype(np.float32)
    ang = np.outer(np.arange(S, dtype=np.float32), freq).astype(np.float32)
    cos, sin = np.cos(ang).astype(np.float32), np.sin(ang).astype(np.float32)
    ropeq = np.zeros((P, 2, 32), np.float32)
    ropeq[KL:, 0, :] = np.concatenate([cos.T, cos.T])
    ropeq[KL:, 1, :] = np.concatenate([sin.T, -sin.T])
    big = np.finfo(np.float32)
    cap = np.where(np.tril(np.ones((S, S), bool)), big.max, big.min).astype(np.float32)
    d = {
        "x": f["x"].reshape(TOK, D),
        "ctxT": f["ctx_4096"].transpose(0, 2, 1).reshape(B, KC, P, CTX).transpose(0, 2, 1, 3),
        "wkT": chunks(f["L0_xattn_Wk"]), "wvT": chunks(f["L0_xattn_Wv"]), "wqT": chunks(f["L0_xattn_Wq"]),
        "woxT": f["L0_xattn_Wo"].T.reshape(H, HD, D).transpose(1, 0, 2),
        "waT": chunks(np.concatenate([f["L0_attn_wq_a"], kva[:KL], kva[KL:][turn]])),
        "wqbn": wqb[:, :NOPE, :].transpose(1, 0, 2),
        "wqra": wqr[:P], "wqrb": wqr[P:],
        "wkn": wkvb[:, :NOPE, :].transpose(1, 0, 2),
        "wvb": wkvb[:, NOPE:, :].transpose(2, 0, 1),
        "wob": f["L0_attn_wo"].T.reshape(NH, VD, D).transpose(1, 0, 2),
        "wfT": chunks(f["L0_ffn_weight"]),
        "bias": f["L0_ffn_bias"].reshape(D), "qnw": f["L0_attn_q_norm_w"], "kvnw": f["L0_attn_kv_norm_w"],
        "ident": np.eye(P, dtype=np.float32),
        "ropek": np.tile(np.stack([cos, sin], 1), (4, 1, 1)), "ropeq": ropeq, "cap": np.tile(cap, (4, 1)),
    }
    return {k: np.ascontiguousarray(v) for k, v in d.items()}


def kernel(**inputs):
    from concourse import bacc
    from concourse.bass_utils import run_bass_kernel_spmd

    nc = bacc.Bacc("TRN2", target_bir_lowering=False, num_devices=1)
    arrays = lay_out({k: np.asarray(v) for k, v in inputs.items()})
    aps = {k: nc.dram_tensor("in_" + k, v.shape, mybir.dt.from_np(v.dtype), kind="ExternalInput").ap()
           for k, v in arrays.items()}
    out = nc.dram_tensor("out_0", (TOK, D), F32, kind="ExternalOutput").ap()
    build(nc, aps, out)
    r = run_bass_kernel_spmd(nc, [{"in_" + k: v for k, v in arrays.items()}], core_ids=[0])
    return r.results[0]["out_0"].reshape(B, S, D)
```

```python
from contextlib import ExitStack

import numpy as np

import concourse.bass as bass
from concourse import mybir

ALU = mybir.AluOpType
ACT = mybir.ActivationFunctionType
AX = mybir.AxisListType
F32 = mybir.dt.float32
F32R = mybir.dt.float32r
F16 = mybir.dt.float16

P = 128
B, S, D = 8, 32, 512
TOK = B * S
TT = TOK // P
KC = D // P
CTX = 512
H, KV, HD = 16, 4, 96
G = H // KV
KVD = KV * HD
KEYS = CTX + S
HALF = KEYS // 2
NK = KVD // P
NV = CTX // P
NU = NK + NV
XSCALE = 1.0 / float(np.sqrt(np.float32(HD)))
NH, NOPE, ROPE, VD = 32, 128, 64, 128
QL, KL = 192, 64
QB = QL - P
LAT = QL + KL + ROPE
MSCALE = 1.0 / float(np.sqrt(np.float32(NOPE + ROPE)))
LN_EPS, RMS_EPS = 1e-5, 1e-6
NHG = NH // 4

B_PROJ, B_S, B_PT, B_O = 0, 2, 4, 6
QBANK = (0, 1, 6, 7)


def blocks_of(j):
    out, r = [], 0
    while r < P:
        head, at = divmod(P * j + r, HD)
        n = min(HD - at, P - r)
        out.append((r, head, at, n))
        r += n
    return out


def build(nc, A, out):
    with ExitStack() as ctx:
        def sb(name, shape, dt=F32, scope=ctx):
            return scope.enter_context(nc.sbuf_tensor(name, shape, dt))

        def sem(name):
            return ctx.enter_context(nc.semaphore(name))

        def overlay(region, nbytes, *groups):
            made = []
            for group in groups:
                with ExitStack() as scope:
                    made.append([sb(n, s, d, scope) for n, s, d in group])
            sb(region, [P, nbytes // 4])
            return made

        ps = ctx.enter_context(nc.psum_tensor("ps", [P, 8, 512], F32))

        xs = sb("xs", [P, TT, D])
        xnT = sb("xnT", [P, KC, TOK])
        ident = sb("ident", [P, P])
        ropek = sb("ropek", [P, 2, 32])
        ropeq = sb("ropeq", [P, 2, 32])
        cap = sb("cap", [P, 32])
        qnw = sb("qnw", [P, QL])
        kvnw = sb("kvnw", [P, KL])
        bias = sb("bias", [P, D], F16)
        small = sb("small", [P, 192])

        (wkh, wkl, wvh, wvl), (wqb,), (wv2, pm) = overlay(
            "r_wkv", 24576,
            [("wkh", [P, KC, KVD], F32R), ("wkl", [P, KC, KVD], F32R),
             ("wvh", [P, KC, KVD], F32R), ("wvl", [P, KC, KVD], F32R)],
            [("wqb", [P, NH, QL], F32)],
            [("wv2", [P, NH, VD], F32), ("pm", [P, 4, 512], F32)])
        (wq,), (wox,), (wo1, wo2) = overlay(
            "r_wq", 32768,
            [("wq", [P, KC, H * HD], F32)], [("wox", [HD, H, D], F32)],
            [("wo1", [P, 8, D], F32), ("wo2", [P, 8, D], F32)])
        (raw,), (wkn,), (qlah, qlal, qlbh, qlbl, t2), (x3h, x3l) = overlay(
            "r_raw", 8192,
            [("raw", [P, KC, CTX], F32)], [("wkn", [P, NH, KL], F32)],
            [("qlah", [P, TOK], F32R), ("qlal", [P, TOK], F32R), ("qlbh", [P, TOK], F32R), ("qlbl", [QB, TOK], F32R),
             ("t2", [P, 2, 512], F32)],
            [("x3h", [P, KC, TOK], F32R), ("x3l", [P, KC, TOK], F32R)])
        (hh0, hl0, hh1, hl1), (wqph, wqpl), (ptm, oc) = overlay(
            "r_half", 32768,
            [("hh0", [P, KC, CTX], F32R), ("hl0", [P, KC, CTX], F32R),
             ("hh1", [P, KC, CTX], F32R), ("hl1", [P, KC, CTX], F32R)],
            [("wqph", [P, NH, P], F32R), ("wqpl", [P, NH, P], F32R)],
            [("ptm", [P, TT, NHG, P], F32), ("oc", [P, 4, NH, S], F32)])
        hh, hl = (hh0, hh1), (hl0, hl1)
        (kt1, v1, kt0, v0), (xh, xl), (_, oh, ol), (qp,), (oTh, oTl, woh, wol) = overlay(
            "r_kv", 32768,
            [("kt1", [HD, KV, KEYS], F32), ("v1", [P, NV + 1, KVD], F32),
             ("kt0", [HD, KV, KEYS], F32), ("v0", [P, NV + 1, KVD], F32)],
            [("xh", [P, KC, TOK], F32R), ("xl", [P, KC, TOK], F32R)],
            [("beside_kv1", [P, 4096], F32), ("oh", [HD, 2, G, TOK], F32R), ("ol", [HD, 2, G, TOK], F32R)],
            [("qp", [P, B, NH, S], F32)],
            [("oTh", [P, 8, TOK], F32R), ("oTl", [P, 8, TOK], F32R),
             ("woh", [P, 4, D], F32R), ("wol", [P, 4, D], F32R)])
        kt, vv = (kt0, kt1), (v0, v1)
        (qT,), (wst,), (wqps,), (wf16, wf) = overlay(
            "r_qT", 16384, [("qT", [HD, H, TOK], F32)], [("wst", [P, 2, KC, KVD], F32)],
            [("wqps", [P, NH, P], F32R)],
            [("wf16", [P, KC, D], F16), ("wf", [P, KC, D], F32R)])
        (outT,), (qst,), (wo0,) = overlay(
            "r_out", 16384, [("outT", [HD, H, TOK], F32)], [("qst", [P, 12, TOK], F32)], [("wo0", [P, 8, D], F32)])
        (kst, qc0, qc1, klat, klst, vlst, pr, pt, pt4), (wra, wrb, wa), (wo3,) = overlay(
            "r_misc", 25216,
            [("kst", [P, NK, CTX], F32), ("qc0", [HD, H, S], F32), ("qc1", [HD, H, S], F32),
             ("klat", [HD, KV, TOK], F32), ("klst", [P, NK, TOK], F32), ("vlst", [P, TT, KVD], F32),
             ("pr", [P, KEYS], F32), ("pt", [P, 512], F32), ("pt4", [S, P], F32)],
            [("wra", [P, NH, ROPE], F32), ("wrb", [QB, NH, ROPE], F32), ("wa", [P, KC, LAT], F32)],
            [("wo3", [P, 8, D], F32)])
        qc = (qc0, qc1)
        wo = (wo0, wo1, wo2, wo3)
        xn = sb("xn", [P, TT, D])
        rope_raw = xn[:, 1, :]
        kp = sb("kp", [P, TT, P])
        bd = sb("bd", [P, TT, 2, P])
        ql = sb("ql", [P, TT, QL])
        kpT = sb("kpT", [P, TOK])
        vlat = nc.dram_tensor("vlat_scratch", [TOK, KVD], F32, kind="Internal").ap()

        s_x, s_const, s_wk, s_wv, s_wq, s_wox = (
            sem(n) for n in ("s_x", "s_const", "s_wk", "s_wv", "s_wq", "s_wox"))
        s_ctx = [sem(f"s_ctx{k}") for k in range(KC)]
        s_wqb, s_wr, s_wrb, s_wv2, s_wf = (sem(n) for n in ("s_wqb", "s_wr", "s_wrb", "s_wv2", "s_wf"))
        s_wo = [sem(f"s_wo{i}") for i in range(4)]
        s_v, s_g = sem("s_v"), sem("s_g")
        s_ks, s_vs = sem("s_ks"), sem("s_vs")
        s_var, s_sd = sem("s_var"), sem("s_sd")
        s_xn = sem("s_xn")
        s_tp, s_xT, s_xs = sem("s_tp"), sem("s_xT"), sem("s_xs")
        s_qh, s_ql = sem("s_qh"), sem("s_ql")
        s_pm, s_pe = sem("s_pm"), sem("s_pe")
        s_kl, s_vl, s_qd = sem("s_kl"), sem("s_vl"), sem("s_qd")
        s_hi, s_lo = sem("s_hi"), sem("s_lo")
        s_ps = sem("s_ps")
        s_kev, s_vev = sem("s_kev"), sem("s_vev")
        s_kt, s_vt = sem("s_kt"), sem("s_vt")
        s_qc = sem("s_qc")
        s_s, s_nm, s_exp, s_pn, s_t, s_pt, s_pt4, s_o, s_oe = (
            sem(n) for n in ("s_s", "s_nm", "s_exp", "s_pn", "s_t", "s_pt", "s_pt4", "s_o", "s_oe"))
        s_wxh, s_wxl, s_os, s_wx = (sem(n) for n in ("s_wxh", "s_wxl", "s_os", "s_wx"))
        s_y = sem("s_y")
        s_res = sem("s_res")
        s_cm, s_ch, s_cl = sem("s_cm"), sem("s_ch"), sem("s_cl")
        s_rh, s_rl = sem("s_rh"), sem("s_rl")
        s_lat, s_sq, s_qk = sem("s_lat"), sem("s_sq"), sem("s_qk")
        s_lt, s_lth, s_ltl, s_bd = sem("s_lt"), sem("s_lth"), sem("s_ltl"), sem("s_bd")
        s_qm, s_qa, s_qv, s_qr, s_qg = (sem(n) for n in ("s_qm", "s_qa", "s_qv", "s_qr", "s_qg"))
        s_ms, s_mx, s_mm, s_me, s_mr, s_mp = (sem(n) for n in ("s_ms", "s_mx", "s_mm", "s_me", "s_mr", "s_mp"))
        s_mt, s_mte, s_pv = sem("s_mt"), sem("s_mte"), sem("s_pv")
        s_pve = [sem("s_pve0"), sem("s_pve1")]
        s_up, s_uph, s_upl = sem("s_up"), sem("s_uph"), sem("s_upl")
        s_woh, s_wol, s_wod = sem("s_woh"), sem("s_wol"), sem("s_wod")
        s_wfc = sem("s_wfc")
        s_out = sem("s_out")

        mv = small[:, 0:4].rearrange("p (t c) -> p t c", t=TT)
        bns = small[:, 4:16].rearrange("p (t c) -> p t c", t=TT)
        va, sd, rr, nt = (small[:, 16 + 4 * i:20 + 4 * i] for i in range(4))
        mx, nm, rs, ri = (small[:, 32 + 4 * i:36 + 4 * i] for i in range(4))
        ssq = small[:, 48:52]
        mmx = [small[:, 64 + 16 * w:80 + 16 * w] for w in range(4)]
        msum = [small[:, 128 + 16 * w:144 + 16 * w] for w in range(4)]

        block = ctx.enter_context(nc.Block())

        NPRO = NK + H * HD // P + TT
        QTILES = H * HD // P
        KDMA = 16 * 7

        @block.sync
        def _(sp):
            sp.dma_start(wst[:, 0], A["wkT"]).then_inc(s_wk, 16)
            for k in range(KC):
                sp.dma_start(raw[:, k, :], A["ctxT"][0][:, k, :]).then_inc(s_ctx[k], 16)
            sp.dma_start(xs[:], A["x"].rearrange("(t p) d -> p t d", p=P)).then_inc(s_x, 16)
            sp.dma_start(wst[:, 1], A["wvT"]).then_inc(s_wv, 16)
            sp.dma_start(wq[:], A["wqT"]).then_inc(s_wq, 16)

            def context(b):
                sp.wait_ge(s_lo, KC * b)
                for k in range(KC):
                    sp.dma_start(raw[:, k, :], A["ctxT"][b][:, k, :]).then_inc(s_ctx[k], 16)

            def keys(b, par):
                for j in range(NK):
                    sp.wait_ge(s_kev, NK * b + j + 1)
                    for r, g, at, n in blocks_of(j):
                        sp.dma_start(kt[par][at:at + n, g, 0:CTX], kst[r:r + n, j, :]).then_inc(s_kt, 16)

            def latents(b, par):
                sp.dma_start(kt[par][:, :, CTX:KEYS], klat[:, :, S * b:S * b + S]).then_inc(s_kt, 16)
                if b == 0:
                    sp.wait_ge(s_vl, 16 * TT)
                sp.dma_start(vv[par][0:S, NV, :], vlat[S * b:S * b + S, :]).then_inc(s_vt, 16)

            keys(0, 0)
            context(1)
            for m in range(NK):
                sp.wait_ge(s_pe, m + 1)
                for r, g, at, n in blocks_of(m):
                    sp.dma_start(klat[at:at + n, g, :], klst[r:r + n, m, :]).then_inc(s_kl, 16)
            sp.wait_ge(s_kl, 16 * 6)
            for m in range(QTILES):
                sp.wait_ge(s_pe, NK + m + 1)
                for r, h, at, n in blocks_of(m):
                    sp.dma_start(qT[at:at + n, h, :], qst[r:r + n, m, :]).then_inc(s_qd, 16)
            for t in range(TT):
                sp.wait_ge(s_pe, NK + QTILES + t + 1)
                sp.dma_start(vlat[P * t:P * t + P, :], vlst[:, t, :]).then_inc(s_vl, 16)
            latents(0, 0)
            context(2)
            sp.dma_start(wox[:], A["woxT"]).then_inc(s_wox, 16)

            for b in range(B):
                if b + 1 < B:
                    if b > 0:
                        sp.wait_ge(s_s, KV * b)
                        sp.wait_ge(s_o, KV * b)
                    keys(b + 1, 1 - b % 2)
                    latents(b + 1, 1 - b % 2)
                if b + 3 < B:
                    context(b + 3)

            sp.wait_ge(s_ps, NU * B)
            sp.dma_start(wqb[:], A["wqbn"]).then_inc(s_wqb, 16)
            sp.dma_start(wkn[:], A["wkn"]).then_inc(s_wqb, 16)
            sp.wait_ge(s_o, KV * B)
            sp.dma_start(wrb[:], A["wqrb"]).then_inc(s_wrb, 16)
            sp.dma_start(wra[:], A["wqra"]).then_inc(s_wr, 16)
            sp.dma_start(wa[:], A["waT"]).then_inc(s_wr, 16)
            sp.wait_ge(s_y, 2)
            sp.dma_start(wo0[:], A["wob"][:, 0:8, :]).then_inc(s_wo[0], 16)
            sp.dma_start(wo1[:], A["wob"][:, 8:16, :]).then_inc(s_wo[1], 16)
            sp.dma_start(wo2[:], A["wob"][:, 16:24, :]).then_inc(s_wo[2], 16)
            sp.wait_ge(s_cm, 4)
            sp.dma_start(wv2[0:KL], A["wvb"]).then_inc(s_wv2, 16)
            sp.dma_start(wv2[KL:P], A["wvb"]).then_inc(s_wv2, 16)
            sp.wait_ge(s_lat, TT)
            sp.wait_ge(s_rl, 2)
            sp.dma_start(wo3[:], A["wob"][:, 24:32, :]).then_inc(s_wo[3], 16)
            sp.wait_ge(s_qm, NH // 2)
            sp.dma_start(wf16[:], A["wfT"]).then_inc(s_wf, 16)
            for t in range(TT):
                sp.wait_ge(s_res, 2 * TT + t + 1)
                sp.dma_start(out[P * t:P * t + P, :], xs[:, t, :]).then_inc(s_out, 16)
            sp.wait_ge(s_out, 16 * TT)

        @block.gpsimd
        def _(pool):
            pool.dma_start(ident[:], A["ident"]).then_inc(s_const, 16)
            pool.dma_start(ropek[:], A["ropek"]).then_inc(s_const, 16)
            pool.dma_start(ropeq[:], A["ropeq"]).then_inc(s_const, 16)
            pool.dma_start(cap[:], A["cap"]).then_inc(s_const, 16)
            pool.dma_start(qnw[:], A["qnw"].partition_broadcast(P)).then_inc(s_const, 16)
            pool.dma_start(kvnw[:], A["kvnw"].partition_broadcast(P)).then_inc(s_const, 16)
            pool.dma_start(bias[:], A["bias"].partition_broadcast(P)).then_inc(s_const, 16)
            pool.memset(bd[:], 0.0).then_inc(s_g, 1)

            def low(b, par, k):
                pool.wait_ge(s_hi, KC * b + k + 1)
                pool.tensor_tensor(hl[par][:, k, :], raw[:, k, :], hh[par][:, k, :], ALU.subtract).then_inc(s_lo, 1)

            def queries(b, par):
                pool.tensor_copy(qc[par][:], qT[:, :, bass.ds(b * S, S)]).then_inc(s_qc, 1)

            def wox_low(g):
                for i in range(G):
                    pool.wait_ge(s_wxh, G * g + i + 1)
                    pool.tensor_tensor(hl[g % 2][0:HD, i, :], wox[:, G * g + i, :], hh[g % 2][0:HD, i, :],
                                       ALU.subtract).then_inc(s_wxl, 1)

            for k in range(KC):
                low(0, 0, k)
            for m in range(QTILES):
                c = slice(P * (m % 4), P * (m % 4) + P)
                pool.wait_ge(s_qh, m + 1)
                pool.tensor_tensor(hl1[:, :, c], wq[:, :, P * m:P * m + P], hh1[:, :, c],
                                   ALU.subtract).then_inc(s_ql, 1)
            pool.wait_ge(s_qd, 16 * 24)
            queries(0, 0)
            for b in range(B):
                if b + 1 < B:
                    if b > 0:
                        pool.wait_ge(s_s, KV * b)
                    queries(b + 1, 1 - b % 2)
                if b + 2 < B:
                    for k in range(KC):
                        low(b + 2, b % 2, k)
            for g in range(KV):
                wox_low(g)

            pool.wait_ge(s_wxl, H)
            pool.wait_ge(s_rh, 1)
            pool.tensor_tensor(wqps[QB:P, :, KL:P], wrb[:], wqps[0:QB, :, KL:P], ALU.subtract).then_inc(s_rl, 1)
            pool.wait_ge(s_rh, 2)
            pool.wait_ge(s_rl, 1)
            pool.tensor_tensor(wqpl[:, :, KL:P], wra[:], wqph[:, :, KL:P], ALU.subtract).then_inc(s_rl, 1)

            def rope_add(lo, hi):
                for n in range(lo, hi):
                    if n % 2 == 0:
                        pool.wait_ge(s_qa, 3 * (n // 2) + 1)
                        if n >= 2:
                            pool.wait_ge(s_qr, n)
                        down = ropeq[KL:KL + 32, 1:2, :].to_broadcast([32, 2 * B, S])
                        pool.tensor_tensor(t2[KL + 32:P, 0, :].rearrange("p (a s) -> p a s", s=S),
                                           rope_raw[KL:KL + 32, :].rearrange("p (a s) -> p a s", s=S),
                                           down, ALU.mult).then_inc(s_qg, 1)
                        pool.wait_ge(s_qg, n // 2 + 1)
                    pool.wait_ge(s_qv, n + 1)
                    rows = qp[KL:P, :, 2 * n:2 * n + 2, :]
                    part = t2[KL:P, n % 2, :].rearrange("p (h b s) -> p b h s", h=2, s=S)
                    pool.tensor_tensor(rows, rows, part, ALU.add).then_inc(s_qr, 1)

            def stat(tile):
                return tile.unsqueeze(2).to_broadcast([P, 16, 32])

            def shift(w):
                sc = pm[:, w, :].rearrange("p (a t) -> p a t", a=16)
                pool.wait_ge(s_mx, w + 1)
                pool.tensor_tensor(sc, sc, stat(mmx[w]), ALU.subtract).then_inc(s_mm, 1)

            def norm(w):
                sc = pm[:, w, :].rearrange("p (a t) -> p a t", a=16)
                pool.wait_ge(s_mr, w + 1)
                pool.tensor_tensor(sc, sc, stat(msum[w]), ALU.mult).then_inc(s_mp, 1)

            pool.wait_ge(s_rl, 2)
            rope_add(0, 8)
            pool.wait_ge(s_qr, 8)
            shift(0)
            pool.wait_ge(s_mm, 1)
            rope_add(8, 12)
            pool.wait_ge(s_qr, 12)
            norm(0)
            shift(1)
            pool.wait_ge(s_mp, 1)
            pool.wait_ge(s_mm, 2)
            rope_add(12, 16)
            pool.wait_ge(s_qr, 16)
            norm(1)
            for h in range(NH):
                pool.wait_ge(s_woh, h + 1)
                pool.tensor_tensor(wol[:, h % 4, :], wo[h // 8][:, h % 8, :], woh[:, h % 4, :],
                                   ALU.subtract).then_inc(s_wol, 1)

        @block.scalar
        def _(act):
            def root(n, lo, hi):
                act.wait_ge(s_var, n)
                act.activation(sd[:, lo:hi], va[:, lo:hi], ACT.Sqrt).then_inc(s_sd, 1)

            def turn_out(n, bank, dst):
                for t in range(TT):
                    act.wait_ge(s_tp, TT * n + t + 1)
                    act.copy(dst[:, :, P * t:P * t + P],
                             ps[:, bank + t, :].rearrange("p (k c) -> p k c", k=KC)).then_inc(s_xT, 1)

            def v_out(b, par, i):
                n = NU * b + NK + i
                act.wait_ge(s_ps, n + 1)
                bank = B_PROJ + (par + NK + i) % 2
                act.copy(vv[par][:, i, :], ps[:, bank, 0:KVD]).then_inc(s_vev, 1)

            root(1, 0, TT)
            for i in range(NV):
                v_out(0, 0, i)
            turn_out(0, B_S, xh)
            for m in range(NPRO):
                act.wait_ge(s_pm, m + 1)
                bank = ps[:, B_PT + m % 4, :]
                if m < NK:
                    dst, src = klst[:, m, :], bank[:, 0:TOK]
                elif m < NK + QTILES:
                    dst, src = qst[:, m - NK, :], bank[:, 0:TOK]
                else:
                    dst, src = vlst[:, m - NK - QTILES, :], bank[:, 0:KVD]
                act.copy(dst, src).then_inc(s_pe, 1)

            for b in range(B):
                more, par = b + 1 < B, b % 2
                for g in range(KV):
                    n = KV * b + g
                    act.wait_ge(s_nm, n + 1)
                    if n > 0:
                        act.wait_ge(s_t, n)
                    act.activation(pr[:].rearrange("p (a k) -> p a k", a=2), ps[:, B_S:B_S + 2, 0:HALF], ACT.Exp,
                                   bias=nm[:, g:g + 1], scale=XSCALE, accum_out=rs[:, g:g + 1]).then_inc(s_exp, 1)
                    if more and g >= 2:
                        v_out(b + 1, 1 - par, 2 * g - NK - 1)
                    act.wait_ge(s_t, n + 1)
                    if n > 0:
                        act.wait_ge(s_o, n)
                    act.copy(pt[:], ps[:, B_PT, :]).then_inc(s_pt, 1)
                    if more and g >= 2:
                        v_out(b + 1, 1 - par, 2 * g - NK)

            act.wait_ge(s_wrb, 16)
            act.copy(wqps[0:QB, :, KL:P], wrb[:]).then_inc(s_rh, 1)
            root(2, 0, TT)

            def absorbed_high(m):
                bank = B_S if m % 2 == 0 else B_O
                act.wait_ge(s_cm, m + 1)
                act.copy(wqph[:, 8 * m:8 * m + 8, 0:KL],
                         ps[:, bank, :].rearrange("p (h c) -> p h c", h=8)).then_inc(s_ch, 1)
                act.copy(wqps[0:QB, 8 * m:8 * m + 8, 0:KL],
                         ps[0:QB, bank + 1, :].rearrange("p (h c) -> p h c", h=8)).then_inc(s_ch, 1)

            act.wait_ge(s_y, TT)
            act.wait_ge(s_wr, 32)
            act.copy(wqph[:, :, KL:P], wra[:]).then_inc(s_rh, 1)
            absorbed_high(0)
            absorbed_high(1)
            turn_out(1, B_PROJ, xnT)
            absorbed_high(2)
            for t in range(TT):
                act.wait_ge(s_lat, t + 1)
                act.activation(xn[:, t, 0:QL], ps[:, B_PT + t, 0:QL], ACT.Square,
                               accum_out=ssq[:, t:t + 1]).then_inc(s_sq, 1)
                act.activation(xn[:, t, QL:QL + KL], ps[:, B_PT + t, QL:QL + KL], ACT.Square,
                               accum_out=ssq[:, TT + t:TT + t + 1]).then_inc(s_sq, 1)
            root(3, 0, 2 * TT)
            absorbed_high(3)
            act.wait_ge(s_lt, 1)
            act.copy(qlah[:], ps[:, B_S, 0:TOK]).then_inc(s_lth, 1)
            act.copy(qlbh[0:QB], ps[0:QB, B_S, TOK:2 * TOK]).then_inc(s_lth, 1)
            act.copy(kpT[:], ps[:, B_S + 1, 0:TOK]).then_inc(s_lth, 1)
            act.wait_ge(s_lth, 2)
            act.copy(qlbh[QB:P], qlbh[0:QB]).then_inc(s_lth, 1)

            def absorbed_out(lo, hi):
                for n in range(lo, hi):
                    act.wait_ge(s_qm, n + 1)
                    if n % 2 == 0:
                        if n >= 2:
                            act.wait_ge(s_qg, n // 2)
                        act.copy(rope_raw[KL:KL + 32, :], ps[KL:KL + 32, QBANK[n % 4], :]).then_inc(s_qa, 1)
                    act.copy(qp[0:KL, :, 2 * n:2 * n + 2, :],
                             ps[0:KL, QBANK[n % 4], :].rearrange("p (h b s) -> p b h s", h=2, s=S)).then_inc(s_qa, 1)

            def exps(w):
                act.wait_ge(s_mm, w + 1)
                act.activation(pm[:, w, :], pm[:, w, :], ACT.Exp, scale=MSCALE).then_inc(s_me, 1)

            def wo_high(h):
                if h % 8 == 0:
                    act.wait_ge(s_wo[h // 8], 16)
                if h >= 4:
                    act.wait_ge(s_wod, h - 3)
                act.copy(woh[:, h % 4, :], wo[h // 8][:, h % 8, :]).then_inc(s_woh, 1)

            absorbed_out(0, 12)
            exps(0)
            absorbed_out(12, 16)
            for w in range(1, 4):
                exps(w)
            act.wait_ge(s_ms, 4)
            for w in range(4):
                act.wait_ge(s_mt, w + 1)
                act.copy(ptm[:, :, 2 * w:2 * w + 2, :],
                         ps[:, B_O + w % 2, :].rearrange("p (t g c) -> p t g c", t=TT, g=2)).then_inc(s_mte, 1)
                wo_high(w)
            for n in range(0, 8, 2):
                act.wait_ge(s_pv, n + 1)
                act.copy(oc[:, n // 2, 0:16, :],
                         ps[:, 0, :].rearrange("p (h s) -> p h s", s=S)).then_inc(s_pve[0], 1)
            for n in range(NH // 4):
                act.wait_ge(s_up, n + 1)
                if n >= 2:
                    act.wait_ge(s_wod, 4 * n - 4)
                for v in range(2):
                    act.copy(oTh[:, 4 * (n % 2):4 * (n % 2) + 4, :].rearrange(
                        "p h (k v s) -> p h k v s", v=2, s=S)[:, :, :, v, :],
                        ps[:, B_S + 2 * (n % 2) + v, :].rearrange("p (h k s) -> p h k s", h=4, s=S)).then_inc(s_uph, 1)
                if n >= 1:
                    for h in range(4 * n, 4 * n + 4):
                        wo_high(h)
            root(4, 0, TT)
            turn_out(2, B_PROJ, x3h)

        @block.vector
        def _(dve):
            chain = [0]

            def link(ins):
                chain[0] += 1
                ins.then_inc(s_v, 1)
                dve.wait_ge(s_v, chain[0])

            def inverse_root(n, lo, hi):
                dve.wait_ge(s_sd, n)
                link(dve.reciprocal(rr[:, lo:hi], sd[:, lo:hi]))
                link(dve.tensor_tensor(nt[:, lo:hi], rr[:, lo:hi], rr[:, lo:hi], ALU.mult))
                link(dve.tensor_tensor(nt[:, lo:hi], nt[:, lo:hi], va[:, lo:hi], ALU.mult))
                link(dve.tensor_scalar(nt[:, lo:hi], nt[:, lo:hi], -0.5, 1.5, ALU.mult, ALU.add))
                link(dve.tensor_tensor(rr[:, lo:hi], rr[:, lo:hi], nt[:, lo:hi], ALU.mult))

            def layernorm(n):
                for t in range(TT):
                    link(dve.bn_stats(bns[:, t, :], xs[:, t, :]))
                    link(dve.bn_aggr(mv[:, t, :], bns[:, t, :]))
                dve.tensor_scalar(va[:, 0:TT], mv[:, :, 1], LN_EPS, None, ALU.add).then_inc(s_var, 1)
                inverse_root(n, 0, TT)
                for t in range(TT):
                    dve.tensor_scalar(xn[:, t, :], xs[:, t, :], mv[:, t, 0:1], rr[:, t:t + 1],
                                      ALU.subtract, ALU.mult).then_inc(s_xn, 1)

            def high(b, par, k):
                dve.wait_ge(s_ctx[k], 16 * (b + 1))
                dve.tensor_copy(hh[par][:, k, :], raw[:, k, :]).then_inc(s_hi, 1)

            def turn_low(n, bank, hi, lo):
                for t in range(TT):
                    c = slice(P * t, P * t + P)
                    dve.wait_ge(s_xT, TT * n + t + 1)
                    dve.tensor_tensor(lo[:, :, c], ps[:, bank + t, :].rearrange("p (k c) -> p k c", k=KC), hi[:, :, c],
                                      ALU.subtract).then_inc(s_xs, 1)

            def k_out(b, par, j):
                dve.wait_ge(s_ps, NU * b + j + 1)
                dve.tensor_copy(kst[:, j, :], ps[:, B_PROJ + (par + j) % 2, :]).then_inc(s_kev, 1)

            dve.wait_ge(s_wk, 16)
            for k in range(KC):
                link(dve.tensor_copy(wkh[:, k, :], wst[:, 0, k, :]))
                dve.tensor_tensor(wkl[:, k, :], wst[:, 0, k, :], wkh[:, k, :], ALU.subtract).then_inc(s_ks, 1)
                high(0, 0, k)
            dve.wait_ge(s_x, 16)
            layernorm(1)
            dve.wait_ge(s_wv, 16)
            for k in range(KC):
                link(dve.tensor_copy(wvh[:, k, :], wst[:, 1, k, :]))
                dve.tensor_tensor(wvl[:, k, :], wst[:, 1, k, :], wvh[:, k, :], ALU.subtract).then_inc(s_vs, 1)
            for j in range(NK):
                k_out(0, 0, j)
            dve.wait_ge(s_wq, 16)

            def wq_high(m):
                if m >= 4:
                    dve.wait_ge(s_pm, NK + m - 3)
                c = slice(P * (m % 4), P * (m % 4) + P)
                dve.tensor_copy(hh1[:, :, c], wq[:, :, P * m:P * m + P]).then_inc(s_qh, 1)

            for m in range(4):
                wq_high(m)
            turn_low(0, B_S, xh, xl)
            for m in range(4, QTILES):
                wq_high(m)
            dve.wait_ge(s_pm, NK + QTILES)
            for k in range(KC):
                high(1, 1, k)
                dve.wait_ge(s_hi, KC + k + 1)
                dve.tensor_tensor(hl1[:, k, :], raw[:, k, :], hh1[:, k, :], ALU.subtract).then_inc(s_lo, 1)

            def o_out(b, g):
                dve.wait_ge(s_o, KV * b + g + 1)
                dve.tensor_copy(outT[:, G * g:G * g + G, bass.ds(b * S, S)],
                                ps[0:HD, B_O + g % 2, 0:P].rearrange("p (h s) -> p h s", h=G)).then_inc(s_oe, 1)

            def o_split(g):
                dve.wait_ge(s_oe, KV * (B - 1) + g + 1)
                if g >= 2:
                    dve.wait_ge(s_wx, g - 1)
                link(dve.tensor_copy(oh[:, g % 2], outT[:, G * g:G * g + G, :]))
                dve.tensor_tensor(ol[:, g % 2], outT[:, G * g:G * g + G, :], oh[:, g % 2], ALU.subtract
                                  ).then_inc(s_os, 1)

            def wox_high(g, i):
                dve.tensor_copy(hh[g % 2][0:HD, i, :], wox[:, G * g + i, :]).then_inc(s_wxh, 1)

            for b in range(B):
                more, ahead, par, last = b + 1 < B, b + 2 < B, b % 2, b == B - 1
                for g in range(KV):
                    n = KV * b + g
                    dve.wait_ge(s_s, n + 1)
                    link(dve.tensor_reduce(mx[:, g:g + 1], ps[:, B_S:B_S + 2, 0:HALF], AX.XY, ALU.max))
                    dve.tensor_scalar(nm[:, g:g + 1], mx[:, g:g + 1], -XSCALE, None, ALU.mult).then_inc(s_nm, 1)
                    if g > 0:
                        o_out(b, g - 1)
                    elif b > 0:
                        o_out(b - 1, KV - 1)
                    if more and g == 1:
                        k_out(b + 1, 1 - par, 1)
                    dve.wait_ge(s_exp, n + 1)
                    link(dve.reciprocal(ri[:, g:g + 1], rs[:, g:g + 1]))
                    dve.tensor_scalar(pr[:], pr[:], ri[:, g:g + 1], None, ALU.mult).then_inc(s_pn, 1)
                    if more and g == 0:
                        dve.wait_ge(s_kt, KDMA * (b + 1))
                        k_out(b + 1, 1 - par, 0)
                    if ahead:
                        if g == 0:
                            dve.wait_ge(s_ps, NU * (b + 1))
                        high(b + 2, par, g)
                    elif not last:
                        if g == 0:
                            dve.wait_ge(s_wox, 16)
                            dve.wait_ge(s_ps, NU * (B - 1))
                        wox_high(0, g)
                    dve.wait_ge(s_t, n + 1)
                    dve.tensor_copy(pt4[:], ps[0:S, B_PT + 1, 0:P]).then_inc(s_pt4, 1)
                    if more and g == 1:
                        k_out(b + 1, 1 - par, 2)
                    if last:
                        if g > 0:
                            o_split(g - 1)
                        if g == 0:
                            dve.wait_ge(s_ps, NU * B)
                        if g >= 2:
                            dve.wait_ge(s_wx, g - 1)
                        if g != 1:
                            for i in range(G):
                                wox_high(max(g, 1), i)
            o_out(B - 1, KV - 1)
            o_split(KV - 1)

            for t in range(TT):
                dve.wait_ge(s_y, t + 1)
                dve.tensor_tensor(xs[:, t, :], xs[:, t, :], ps[:, B_PROJ + t, :], ALU.add).then_inc(s_res, 1)
            dve.wait_ge(s_res, TT)
            layernorm(2)

            def absorbed_low(m):
                bank = B_S if m % 2 == 0 else B_O
                r = slice(8 * m, 8 * m + 8)
                dve.wait_ge(s_ch, 2 * m + 2)
                dve.tensor_tensor(wqpl[:, r, 0:KL], ps[:, bank, :].rearrange("p (h c) -> p h c", h=8),
                                  wqph[:, r, 0:KL], ALU.subtract).then_inc(s_cl, 1)
                dve.tensor_tensor(wqps[QB:P, r, 0:KL], ps[0:QB, bank + 1, :].rearrange("p (h c) -> p h c", h=8),
                                  wqps[0:QB, r, 0:KL], ALU.subtract).then_inc(s_cl, 1)

            for m in range(3):
                absorbed_low(m)
            dve.wait_ge(s_sq, 2 * TT)
            link(dve.tensor_scalar(va[:, 0:TT], ssq[:, 0:TT], 1.0 / QL, RMS_EPS, ALU.mult, ALU.add))
            dve.tensor_scalar(va[:, TT:2 * TT], ssq[:, TT:2 * TT], 1.0 / KL, RMS_EPS,
                              ALU.mult, ALU.add).then_inc(s_var, 1)
            inverse_root(3, 0, 2 * TT)
            for t in range(TT):
                lat = ps[:, B_PT + t, :]
                dve.scalar_tensor_tensor(out=ql[:, t, :], in0=lat[:, 0:QL], scalar=rr[:, t:t + 1], in1=qnw[:],
                                         op0=ALU.mult, op1=ALU.mult).then_inc(s_qk, 1)
            for t in range(TT):
                lat = ps[:, B_PT + t, :]
                link(dve.scalar_tensor_tensor(out=kp[:, t, 0:KL], in0=lat[:, QL:QL + KL],
                                              scalar=rr[:, TT + t:TT + t + 1], in1=kvnw[:],
                                              op0=ALU.mult, op1=ALU.mult))
            x1 = ps[:, B_PT:B_PT + TT, QL + KL:QL + KL + 32]
            x2 = ps[:, B_PT:B_PT + TT, QL + KL + 32:LAT]
            cos, sin = (ropek[:, i:i + 1, :].to_broadcast([P, TT, 32]) for i in range(2))
            rot = xn[:, 0, 256:512].rearrange("p (a t c) -> p a t c", a=4, t=TT)
            for i, (a, w) in enumerate(((x1, cos), (x2, sin), (x1, sin), (x2, cos))):
                link(dve.tensor_tensor(rot[:, i], a, w, ALU.mult))
            dve.tensor_tensor(kp[:, :, KL:KL + 32], rot[:, 0], rot[:, 1], ALU.subtract).then_inc(s_qk, 1)
            dve.tensor_tensor(kp[:, :, KL + 32:P], rot[:, 2], rot[:, 3], ALU.add).then_inc(s_qk, 1)
            absorbed_low(3)
            dve.wait_ge(s_lth, 2)
            dve.tensor_tensor(qlal[:], ps[:, B_S, 0:TOK], qlah[:], ALU.subtract).then_inc(s_ltl, 1)
            dve.tensor_tensor(qlbl[:], ps[0:QB, B_S, TOK:2 * TOK], qlbh[0:QB], ALU.subtract).then_inc(s_ltl, 1)

            def rope(lo, hi):
                for n in range(lo, hi):
                    dve.wait_ge(s_qm, n + 1)
                    if n >= 2:
                        dve.wait_ge(s_qr, n - 1)
                    q = ps[:, QBANK[n % 4], :].rearrange("p (a s) -> p a s", s=S)
                    qb = ps[:, QBANK[n % 4], :].rearrange("p (h b s) -> p b h s", h=2, s=S)
                    tt = t2[:, n % 2, :].rearrange("p (a s) -> p a s", s=S)
                    cosb = ropeq[KL:P, 0:1, :].unsqueeze(1).to_broadcast([P - KL, B, 2, S])
                    up, down = (ropeq[r:r + 32, 1:2, :].to_broadcast([32, 2 * B, S]) for r in (KL + 32, KL))
                    dve.tensor_tensor(tt[KL:KL + 32], q[KL + 32:P], up, ALU.mult).then_inc(s_v, 1)
                    chain[0] += 1
                    if n % 2:
                        dve.tensor_tensor(tt[KL + 32:P], q[KL:KL + 32], down, ALU.mult).then_inc(s_v, 1)
                        chain[0] += 1
                    else:
                        dve.wait_ge(s_qa, 3 * (n // 2) + 1)
                    dve.tensor_tensor(qp[KL:P, :, 2 * n:2 * n + 2, :], qb[KL:P], cosb, ALU.mult).then_inc(s_qv, 1)

            capb = cap[:].unsqueeze(1).to_broadcast([P, 16, 32])

            def largest(w):
                sc = pm[:, w, :].rearrange("p (a t) -> p a t", a=16)
                dve.wait_ge(s_ms, w + 1)
                link(dve.tensor_tensor(sc, ps[:, B_S + w, :].rearrange("p (a t) -> p a t", a=16), capb, ALU.min))
                dve.tensor_reduce(mmx[w], sc, AX.X, ALU.max).then_inc(s_mx, 1)

            def total(w):
                dve.wait_ge(s_me, w + 1)
                link(dve.tensor_reduce(msum[w], pm[:, w, :].rearrange("p (a t) -> p a t", a=16), AX.X, ALU.add))
                dve.reciprocal(msum[w], msum[w]).then_inc(s_mr, 1)

            def blockdiag():
                dve.wait_ge(s_g, 1)
                for u in range(4):
                    r = slice(S * u, S * u + S)
                    dve.tensor_copy(bd[r, :, u // 2, KL * (u % 2):KL * (u % 2) + KL], kp[r, :, 0:KL]).then_inc(s_bd, 1)

            rope(0, 8)
            largest(0)
            rope(8, 12)
            total(0)
            largest(1)
            rope(12, 16)
            blockdiag()
            largest(2)
            total(1)
            for w in range(2, 4):
                sc = pm[:, w, :].rearrange("p (a t) -> p a t", a=16)
                if w == 3:
                    largest(3)
                dve.wait_ge(s_mx, w + 1)
                if w == 2:
                    dve.wait_ge(s_mm, 2)
                dve.tensor_tensor(sc, sc, mmx[w].unsqueeze(2).to_broadcast([P, 16, 32]), ALU.subtract
                                  ).then_inc(s_mm, 1)
            for w in range(2, 4):
                sc = pm[:, w, :].rearrange("p (a t) -> p a t", a=16)
                total(w)
                dve.wait_ge(s_mr, w + 1)
                dve.wait_ge(s_mp, w)
                dve.tensor_tensor(sc, sc, msum[w].unsqueeze(2).to_broadcast([P, 16, 32]), ALU.mult
                                  ).then_inc(s_mp, 1)
            for n in range(1, 8, 2):
                dve.wait_ge(s_pv, n + 1)
                dve.tensor_copy(oc[:, n // 2, 16:32, :],
                                ps[:, 1, :].rearrange("p (h s) -> p h s", s=S)).then_inc(s_pve[1], 1)
            for n in range(NH // 4):
                dve.wait_ge(s_uph, 2 * n + 2)
                for v in range(2):
                    ring = [x[:, 4 * (n % 2):4 * (n % 2) + 4, :].rearrange(
                        "p h (k v s) -> p h k v s", v=2, s=S)[:, :, :, v, :] for x in (oTh, oTl)]
                    dve.tensor_tensor(ring[1], ps[:, B_S + 2 * (n % 2) + v, :].rearrange(
                        "p (h k s) -> p h k s", h=4, s=S), ring[0], ALU.subtract).then_inc(s_upl, 1)
            dve.wait_ge(s_wf, 16)
            dve.tensor_copy(wf[:], wf16[:]).then_inc(s_wfc, 1)
            for t in range(TT):
                dve.wait_ge(s_y, TT + t + 1)
                dve.tensor_tensor(xs[:, t, :], xs[:, t, :], ps[:, B_O + t, :], ALU.add).then_inc(s_res, 1)
            dve.wait_ge(s_res, 2 * TT)
            layernorm(4)
            for t in range(TT):
                link(dve.tensor_tensor(xs[:, t, :], xs[:, t, :], bias[:], ALU.add))
            turn_low(2, B_PROJ, x3h, x3l)
            for t in range(TT):
                dve.wait_ge(s_y, 2 * TT + t + 1)
                dve.tensor_tensor(xs[:, t, :], xs[:, t, :], ps[:, B_S + t, :], ALU.add).then_inc(s_res, 1)

        @block.tensor
        def _(pe):
            def three(o, stationary, moving, first, last):
                (wh, wl), (mh, ml) = stationary, moving
                for i, (w, m) in enumerate(((wh, mh), (wl, mh), (wh, ml))):
                    mm = pe.matmul(o, w, m, start=first and i == 0, stop=last and i == 2)
                return mm

            def project(b, par, first, last):
                for step in range(first, last):
                    u, k = step // KC, step % KC
                    bank = B_PROJ + (par + u) % 2
                    if step < KC:
                        pe.wait_ge(s_lo, KC * b + (k + 1 if b == 0 else KC))
                    if b == 0 and u == 0:
                        pe.wait_ge(s_ks, k + 1)
                    if b == 0 and u == NK:
                        pe.wait_ge(s_vs, k + 1)
                    if k == 0:
                        if u < 2 and b > 0:
                            pe.wait_ge(s_vev, NV * (b - 1) + 3 + u)
                        elif 2 <= u < NK + 2:
                            pe.wait_ge(s_kev, NK * b + u - 1)
                        elif u >= NK + 2:
                            pe.wait_ge(s_vev, NV * b + u - NK - 1)
                    if u < NK:
                        c = slice(P * u, P * u + P)
                        mm = three(ps[:, bank, :], (wkh[:, k, c], wkl[:, k, c]),
                                   (hh[par][:, k, :], hl[par][:, k, :]), k == 0, k == KC - 1)
                    else:
                        c = slice(P * (u - NK), P * (u - NK) + P)
                        mm = three(ps[:, bank, 0:KVD], (hh[par][:, k, c], hl[par][:, k, c]),
                                   (wvh[:, k, :], wvl[:, k, :]), k == 0, k == KC - 1)
                    if k == KC - 1:
                        mm.then_inc(s_ps, 1)

            def turn(n, bank):
                for t in range(TT):
                    pe.wait_ge(s_xn, TT * n + t + 1)
                    for k in range(KC):
                        tr = pe.transpose(ps[:, bank + t, P * k:P * k + P], xn[:, t, P * k:P * k + P], ident[:])
                    tr.then_inc(s_tp, 1)

            project(0, 0, 0, NU * KC)
            pe.wait_ge(s_const, 16 * 7)
            turn(0, B_S)
            pe.wait_ge(s_xs, TT)
            for m in range(NPRO):
                if m >= 4:
                    pe.wait_ge(s_pe, m - 3)
                bank = B_PT + m % 4
                for k in range(KC):
                    ends = (k == 0, k == KC - 1)
                    if m < NK:
                        c = slice(P * m, P * m + P)
                        mm = three(ps[:, bank, 0:TOK], (wkh[:, k, c], wkl[:, k, c]), (xh[:, k, :], xl[:, k, :]), *ends)
                    elif m < NK + QTILES:
                        q = m - NK
                        if k == 0:
                            pe.wait_ge(s_ql, q + 1)
                        c = slice(P * (q % 4), P * (q % 4) + P)
                        mm = three(ps[:, bank, 0:TOK], (hh1[:, k, c], hl1[:, k, c]), (xh[:, k, :], xl[:, k, :]), *ends)
                    else:
                        t = m - NK - QTILES
                        c = slice(P * t, P * t + P)
                        mm = three(ps[:, bank, 0:KVD], (xh[:, k, c], xl[:, k, c]), (wvh[:, k, :], wvl[:, k, :]), *ends)
                mm.then_inc(s_pm, 1)

            def scores(b, par, g):
                if g == 0:
                    pe.wait_ge(s_qc, b + 1)
                    pe.wait_ge(s_kt, KDMA * (b + 1))
                for a in range(2):
                    mm = pe.matmul(ps[:, B_S + a, 0:HALF], qc[par][:, G * g:G * g + G, :].rearrange("p h s -> p (h s)"),
                                   kt[par][:, g, HALF * a:HALF * a + HALF], start=True, stop=True)
                mm.then_inc(s_s, 1)

            def wox_group(g, first, last):
                pe.wait_ge(s_os, g + 1)
                for i in range(first, last):
                    pe.wait_ge(s_wxl, G * g + i + 1)
                    for t in range(TT):
                        c = slice(P * t, P * t + P)
                        mm = three(ps[:, B_PROJ + t, :], (oh[:, g % 2, i, c], ol[:, g % 2, i, c]),
                                   (hh[g % 2][0:HD, i, :], hl[g % 2][0:HD, i, :]),
                                   g == 0 and i == 0, g == KV - 1 and i == G - 1)
                        if g == KV - 1 and i == G - 1:
                            mm.then_inc(s_y, 1)
                if g < KV - 1 and last == G:
                    mm.then_inc(s_wx, 1)

            CUTS = [0, 4, 7, 11, 14, 18, 21, 25, 28]
            scores(0, 0, 0)
            for b in range(B):
                more, par = b + 1 < B, b % 2
                for g in range(KV):
                    n = KV * b + g
                    if more:
                        project(b + 1, 1 - par, CUTS[2 * g], CUTS[2 * g + 1])
                    pe.wait_ge(s_pn, n + 1)
                    if n > 0:
                        pe.wait_ge(s_pt, n)
                        pe.wait_ge(s_pt4, n)
                    for j in range(NV):
                        pe.transpose(ps[:, B_PT, P * j:P * j + P], pr[:, P * j:P * j + P], ident[:])
                    pe.transpose(ps[0:S, B_PT + 1, 0:P], pr[:, CTX:KEYS], ident[:]).then_inc(s_t, 1)
                    if more:
                        project(b + 1, 1 - par, CUTS[2 * g + 1], CUTS[2 * g + 2])
                    if g + 1 < KV:
                        scores(b, par, g + 1)
                    elif more:
                        scores(b + 1, 1 - par, 0)
                    if not more and g > 0:
                        if g == 1:
                            pe.wait_ge(s_vev, NV * B)
                        wox_group(g - 1, 0, 1)
                    pe.wait_ge(s_pt, n + 1)
                    pe.wait_ge(s_pt4, n + 1)
                    if g == 0:
                        pe.wait_ge(s_vev, NV * (b + 1))
                        pe.wait_ge(s_vt, 16 * (b + 1))
                    if n > 1:
                        pe.wait_ge(s_oe, n - 1)
                    o = ps[0:HD, B_O + g % 2, 0:P]
                    for j in range(NV):
                        pe.matmul(o, vv[par][:, j, HD * g:HD * g + HD], pt[:, P * j:P * j + P], start=(j == 0), stop=False)
                    pe.matmul(o, vv[par][0:S, NV, HD * g:HD * g + HD], pt4[:], start=False, stop=True).then_inc(s_o, 1)
                    if not more and g > 0:
                        wox_group(g - 1, 1, G)
            wox_group(KV - 1, 0, G)

            def absorb(m):
                bank = B_S if m % 2 == 0 else B_O
                if m >= 2:
                    pe.wait_ge(s_cl, 2 * (m - 1))
                for i in range(8):
                    h = 8 * m + i
                    pe.matmul(ps[:, bank, KL * i:KL * i + KL], wqb[:, h, 0:P], wkn[:, h, :], start=True, stop=True)
                    mm = pe.matmul(ps[0:QB, bank + 1, KL * i:KL * i + KL], wqb[:, h, P:QL], wkn[:, h, :],
                                   start=True, stop=True)
                mm.then_inc(s_cm, 1)

            pe.wait_ge(s_wqb, 32)
            pe.wait_ge(s_oe, KV * B)
            absorb(0)
            absorb(1)
            turn(1, B_PROJ)
            absorb(2)
            pe.wait_ge(s_wr, 32)
            pe.wait_ge(s_xT, 2 * TT)
            for t in range(TT):
                for k in range(KC):
                    mm = pe.matmul(ps[:, B_PT + t, 0:LAT], xnT[:, k, P * t:P * t + P], wa[:, k, :],
                                   start=(k == 0), stop=(k == KC - 1))
                mm.then_inc(s_lat, 1)
            absorb(3)
            pe.wait_ge(s_qk, TT + 2)
            pe.wait_ge(s_cl, 6)
            for t in range(TT):
                pe.transpose(ps[:, B_S, P * t:P * t + P], ql[:, t, 0:P], ident[:])
                pe.transpose(ps[0:QB, B_S, TOK + P * t:TOK + P * t + P], ql[:, t, P:QL], ident[:])
                tr = pe.transpose(ps[:, B_S + 1, P * t:P * t + P], kp[:, t, :], ident[:])
            tr.then_inc(s_lt, 1)
            pe.wait_ge(s_cl, 8)
            pe.wait_ge(s_rl, 2)
            pe.wait_ge(s_lth, 4)
            pe.wait_ge(s_ltl, 2)

            def copies(n):
                return 3 * (n // 2) + (3 if n % 2 else 2)

            def queries(lo, hi):
                for n in range(lo, hi):
                    if n >= 4:
                        pe.wait_ge(s_qa, copies(n - 4))
                        pe.wait_ge(s_qv, n - 3)
                    for i in range(2):
                        h = 2 * n + i
                        o = ps[:, QBANK[n % 4], TOK * i:TOK * i + TOK]
                        three(o, (wqph[:, h, :], wqpl[:, h, :]), (qlah[:], qlal[:]), True, False)
                        pe.matmul(o, wqps[:, h, :], qlbh[:], start=False, stop=False)
                        mm = pe.matmul(o, wqps[0:QB, h, :], qlbl[:], start=False, stop=True)
                    mm.then_inc(s_qm, 1)

            def latent_scores(w):
                pe.wait_ge(s_qa, copies(4 * w + 3))
                pe.wait_ge(s_qr, 4 * w + 4)
                for i in range(2):
                    for b in range(B):
                        g = 2 * w + i
                        mm = pe.matmul(ps[:, B_S + w, S * (B * i + b):S * (B * i + b) + S],
                                       qp[:, b, 4 * g:4 * g + 4, :].rearrange("p h s -> p (h s)"),
                                       kpT[:, S * b:S * b + S], start=True, stop=True)
                mm.then_inc(s_ms, 1)

            queries(0, 8)
            latent_scores(0)
            queries(8, 12)
            latent_scores(1)
            queries(12, 16)
            latent_scores(2)
            latent_scores(3)
            for w in range(4):
                pe.wait_ge(s_mp, w + 1)
                if w >= 2:
                    pe.wait_ge(s_mte, w - 1)
                for t in range(TT):
                    for i in range(2):
                        at = B * S * i + P * t
                        tr = pe.transpose(ps[:, B_O + w % 2, P * (2 * t + i):P * (2 * t + i) + P],
                                          pm[:, w, at:at + P], ident[:])
                tr.then_inc(s_mt, 1)
            pe.wait_ge(s_mte, 4)
            pe.wait_ge(s_bd, 4)
            for n in range(8):
                if n >= 2:
                    pe.wait_ge(s_pve[n % 2], n // 2)
                tq, half = n // 2, n % 2
                pe.matmul(ps[:, n % 2, :], bd[:, tq // 2, tq % 2, :], ptm[:, tq // 2, 4 * half:4 * half + 4, :],
                          start=True, stop=True).then_inc(s_pv, 1)
            for copied in s_pve:
                pe.wait_ge(copied, 4)
            pe.wait_ge(s_wv2, 32)

            def up(n):
                if n >= 2:
                    pe.wait_ge(s_upl, 2 * n - 2)
                for v in range(2):
                    for i in range(4):
                        mm = pe.matmul(ps[:, B_S + 2 * (n % 2) + v, P * i:P * i + P],
                                       wv2[KL * v:KL * v + KL, 4 * n + i, :], oc[KL * v:KL * v + KL, :, 4 * n + i, :],
                                       start=True, stop=True)
                mm.then_inc(s_up, 1)

            up(0)
            up(1)
            for n in range(NH // 4):
                pe.wait_ge(s_upl, 2 * n + 2)
                for h in range(4 * n, 4 * n + 4):
                    pe.wait_ge(s_wol, h + 1)
                    for t in range(TT):
                        c = slice(P * t, P * t + P)
                        mm = three(ps[:, B_O + t, :], (oTh[:, h % 8, c], oTl[:, h % 8, c]),
                                   (woh[:, h % 4, :], wol[:, h % 4, :]), h == 0, h == NH - 1)
                        if h == NH - 1:
                            mm.then_inc(s_y, 1)
                    if h < NH - 1:
                        mm.then_inc(s_wod, 1)
                if n + 2 < NH // 4:
                    up(n + 2)
            turn(2, B_PROJ)
            pe.wait_ge(s_wfc, 1)
            pe.wait_ge(s_xs, 2 * TT)
            for t in range(TT):
                c = slice(P * t, P * t + P)
                for k in range(KC):
                    for half in (x3h, x3l):
                        mm = pe.matmul(ps[:, B_S + t, :], half[:, k, c], wf[:, k, :],
                                       start=(k == 0 and half is x3h), stop=(k == KC - 1 and half is x3l))
                mm.then_inc(s_y, 1)


def lay_out(a):
    f = {k: np.ascontiguousarray(v) for k, v in a.items()}

    def chunks(w):
        return w.T.reshape(KC, P, w.shape[0]).transpose(1, 0, 2)

    turn = np.concatenate([np.arange(0, ROPE, 2), np.arange(1, ROPE, 2)])
    kva = f["L0_attn_wkv_a"]
    wqb = f["L0_attn_wq_b"].reshape(NH, NOPE + ROPE, QL)
    wkvb = f["L0_attn_wkv_b"].reshape(NH, NOPE + VD, KL)
    wqr = wqb[:, NOPE:, :][:, turn, :].transpose(2, 0, 1)
    freq = (1.0 / 10000.0 ** (np.arange(0, ROPE, 2, dtype=np.float32) / np.float32(ROPE))).astype(np.float32)
    ang = np.outer(np.arange(S, dtype=np.float32), freq).astype(np.float32)
    cos, sin = np.cos(ang).astype(np.float32), np.sin(ang).astype(np.float32)
    ropeq = np.zeros((P, 2, 32), np.float32)
    ropeq[KL:, 0, :] = np.concatenate([cos.T, cos.T])
    ropeq[KL:, 1, :] = np.concatenate([sin.T, -sin.T])
    big = np.finfo(np.float32)
    cap = np.where(np.tril(np.ones((S, S), bool)), big.max, big.min).astype(np.float32)
    d = {
        "x": f["x"].reshape(TOK, D),
        "ctxT": f["ctx_4096"].transpose(0, 2, 1).reshape(B, KC, P, CTX).transpose(0, 2, 1, 3),
        "wkT": chunks(f["L0_xattn_Wk"]), "wvT": chunks(f["L0_xattn_Wv"]), "wqT": chunks(f["L0_xattn_Wq"]),
        "woxT": f["L0_xattn_Wo"].T.reshape(H, HD, D).transpose(1, 0, 2),
        "waT": chunks(np.concatenate([f["L0_attn_wq_a"], kva[:KL], kva[KL:][turn]])),
        "wqbn": wqb[:, :NOPE, :].transpose(1, 0, 2),
        "wqra": wqr[:P], "wqrb": wqr[P:],
        "wkn": wkvb[:, :NOPE, :].transpose(1, 0, 2),
        "wvb": wkvb[:, NOPE:, :].transpose(2, 0, 1),
        "wob": f["L0_attn_wo"].T.reshape(NH, VD, D).transpose(1, 0, 2),
        "wfT": chunks(f["L0_ffn_weight"]),
        "bias": f["L0_ffn_bias"].reshape(D), "qnw": f["L0_attn_q_norm_w"], "kvnw": f["L0_attn_kv_norm_w"],
        "ident": np.eye(P, dtype=np.float32),
        "ropek": np.tile(np.stack([cos, sin], 1), (4, 1, 1)), "ropeq": ropeq, "cap": np.tile(cap, (4, 1)),
    }
    return {k: np.ascontiguousarray(v) for k, v in d.items()}


def kernel(**inputs):
    from concourse import bacc
    from concourse.bass_utils import run_bass_kernel_spmd

    nc = bacc.Bacc("TRN2", target_bir_lowering=False, num_devices=1)
    arrays = lay_out({k: np.asarray(v) for k, v in inputs.items()})
    aps = {k: nc.dram_tensor("in_" + k, v.shape, mybir.dt.from_np(v.dtype), kind="ExternalInput").ap()
           for k, v in arrays.items()}
    out = nc.dram_tensor("out_0", (TOK, D), F32, kind="ExternalOutput").ap()
    build(nc, aps, out)
    r = run_bass_kernel_spmd(nc, [{"in_" + k: v for k, v in arrays.items()}], core_ids=[0])
    return r.results[0]["out_0"].reshape(B, S, D)
```

```python
from contextlib import ExitStack

import numpy as np

import concourse.bass as bass
from concourse import mybir

ALU = mybir.AluOpType
ACT = mybir.ActivationFunctionType
AX = mybir.AxisListType
F32 = mybir.dt.float32
F32R = mybir.dt.float32r
F16 = mybir.dt.float16

P = 128
B, S, D = 8, 32, 512
TOK = B * S
TT = TOK // P
KC = D // P
CTX = 512
H, KV, HD = 16, 4, 96
G = H // KV
KVD = KV * HD
KEYS = CTX + S
HALF = KEYS // 2
NK = KVD // P
NV = CTX // P
NU = NK + NV
OT = H * HD // P
OG = OT // KV
XSCALE = 1.0 / float(np.sqrt(np.float32(HD)))
NH, NOPE, ROPE, VD = 32, 128, 64, 128
QL, KL = 192, 64
QB = QL - P
LAT = QL + KL + ROPE
MSCALE = 1.0 / float(np.sqrt(np.float32(NOPE + ROPE)))
LN_EPS, RMS_EPS = 1e-5, 1e-6
PAIRS = (B - 4) // 2
NHG = NH // 4

WARM = 5

WEIGHTED = ((0, 0), (1, 0), (0, 1), (1, 1), (2, 0), (3, 0), (2, 1), (3, 1))

B_PROJ, B_S, B_PT, B_O = 0, 2, 4, 6
QBANK = (0, 1, 6, 7)
NPAIR = NH // 2


def is_first(b):
    return isinstance(b, int) and b == 0


def left(b):
    return B - 1 - b if isinstance(b, int) else B


def each_batch(engine, step):
    step(0, 0)
    with engine.Fori(0, PAIRS) as i:
        for u in (1, 2):
            step(2 * i + u, u % 2)
    for b in range(2 * PAIRS + 1, B):
        step(b, b % 2)


def blocks_of(j):
    out, r = [], 0
    while r < P:
        head, at = divmod(P * j + r, HD)
        n = min(HD - at, P - r)
        out.append((r, head, at, n))
        r += n
    return out


def bits(halves):
    return halves.bitcast(F32)


def build(nc, A, out):
    with ExitStack() as ctx:
        def sb(name, shape, dt=F32, scope=ctx):
            return scope.enter_context(nc.sbuf_tensor(name, shape, dt))

        def sem(name):
            return ctx.enter_context(nc.semaphore(name))

        def overlay(region, nbytes, *groups):
            made = []
            for group in groups:
                with ExitStack() as scope:
                    made.append([sb(n, s, d, scope) for n, s, d in group])
            sb(region, [P, nbytes // 4])
            return made

        ps = ctx.enter_context(nc.psum_tensor("ps", [P, 8, 512], F32))

        xs = sb("xs", [P, TT, D])
        (xnT,), (xh,) = overlay("r_xn", 4096, [("xnT", [P, KC, TOK], F32)],
                                [("xh", [P, KC, TOK], F32R)])
        ident = sb("ident", [P, P])
        ropek = sb("ropek", [P, 2, 32])
        ropeq = sb("ropeq", [P, 2, 32])
        cap = sb("cap", [P, 32])
        qnw = sb("qnw", [P, QL])
        kvnw = sb("kvnw", [P, KL])
        bias = sb("bias", [P, D], F16)
        small = sb("small", [P, 192])

        (wkh, wkl, wvh, wvl), (wqb,), (wvn, pm) = overlay(
            "r_wkv", 24576,
            [("wkh", [P, KC, KVD], F32R), ("wkl", [P, KC, KVD], F32R),
             ("wvh", [P, KC, KVD], F32R), ("wvl", [P, KC, KVD], F32R)],
            [("wqb", [P, NH, QL], F32)],
            [("wvn", [P, NH, KL], F32), ("pm", [P, 4, 512], F32)])
        (wq,), (kt1, v1, qc1, vlst), (wo1, wo2), (wc1, wc2) = overlay(
            "r_wq", 32768,
            [("wq", [P, KC, H * HD], F32)],
            [("kt1", [HD, 2, KV, KEYS], F32R), ("v1", [P, NV + 1, KVD], F32), ("qc1", [HD, 2, H, S], F32R),
             ("vlst", [P, TT, KVD], F32)],
            [("wo1", [P, 8, D], F32), ("wo2", [P, 8, D], F32)],
            [("wc1", [P, 8, D], F32R), ("wc2", [P, 8, D], F32R)])
        (raw,), (woxa,), (wkn,), (qlah, qlal, qlbh, qlbl, t2), (x3h, x3l) = overlay(
            "r_raw", 8192,
            [("raw", [P, KC, CTX], F32)], [("woxa", [P, OG, D], F32)], [("wkn", [P, NH, KL], F32)],
            [("qlah", [P, TOK], F32R), ("qlal", [P, TOK], F32R), ("qlbh", [P, TOK], F32R), ("qlbl", [QB, TOK], F32R),
             ("t2", [P, 2, 512], F32)],
            [("x3h", [P, KC, TOK], F32R), ("x3l", [P, KC, TOK], F32R)])
        (hh0, hl0, hh1, hl1), (wqph, wqpl), (ptm,) = overlay(
            "r_half", 32768,
            [("hh0", [P, KC, CTX], F32R), ("hl0", [P, KC, CTX], F32R),
             ("hh1", [P, KC, CTX], F32R), ("hl1", [P, KC, CTX], F32R)],
            [("wqph", [P, NH, P], F32R), ("wqpl", [P, NH, P], F32R)],
            [("ptm", [P, TT, NHG, P], F32)])
        hh, hl = (hh0, hh1), (hl0, hl1)
        (kt0, v0, xl), (oh, ol), (qp,), (och, ocl) = overlay(
            "r_kv", 32768,
            [("kt0", [HD, 2, KV, KEYS], F32R), ("v0", [P, NV + 1, KVD], F32), ("xl", [P, KC, TOK], F32R)],
            [("oh", [P, 2, OG, TOK], F32R), ("ol", [P, 2, OG, TOK], F32R)],
            [("qp", [P, B, NH, S], F32)],
            [("och", [P, NH // 2, TOK], F32R), ("ocl", [P, NH // 2, TOK], F32R)])
        kt, vv = (kt0, kt1), (v0, v1)
        (qT,), (wst,), (klst,), (woxb,), (wqps,), (wf16, wf) = overlay(
            "r_qT", 16384, [("qT", [HD, H, TOK], F32)], [("wst", [P, 2, KC, KVD], F32)],
            [("klst", [P, 2, NK, TOK], F32R)], [("woxb", [P, 2, OG, D], F32)],
            [("wqps", [P, NH, P], F32R)],
            [("wf16", [P, KC, D], F16), ("wf", [P, KC, D], F32R)])
        (outT, qc0), (qst,), (wo0,), (wc0,) = overlay(
            "r_out", 16384, [("outT", [P, OT, TOK], F32), ("qc0", [HD, 2, H, S], F32R)],
            [("qst", [P, 12, TOK], F32)], [("wo0", [P, 8, D], F32)],
            [("wc0", [P, 8, D], F32R)])
        (kst, klat, pr, pt, pt4), (wra, wrb, wa), (wo3,), (wc3,) = overlay(
            "r_misc", 25216,
            [("kst", [P, 2, NK, CTX], F32R), ("klat", [HD, 2, KV, TOK], F32R),
             ("pr", [P, KEYS], F32), ("pt", [P, 512], F32), ("pt4", [S, P], F32)],
            [("wra", [P, NH, ROPE], F32), ("wrb", [QB, NH, ROPE], F32), ("wa", [P, KC, LAT], F32)],
            [("wo3", [P, 8, D], F32)], [("wc3", [P, 8, D], F32R)])
        qc = (qc0, qc1)
        wox = (woxa, woxa, woxb[:, 0], woxb[:, 1])
        wo = (wo0, wo1, wo2, wo3)
        wc = (wc0, wc1, wc2, wc3)
        xn = sb("xn", [P, TT, D])
        rope_raw = xn[:, 1, :]
        kp = sb("kp", [P, TT, P])
        bd = sb("bd", [P, TT, 2, P])
        ql = sb("ql", [P, TT, QL])
        kpT = sb("kpT", [P, TOK])
        vlat = nc.dram_tensor("vlat_scratch", [TOK, KVD], F32, kind="Internal").ap()

        QPARTS = H * HD // 512
        s_x, s_const, s_wv = (sem(n) for n in ("s_x", "s_const", "s_wv"))
        s_wox = [sem(f"s_wox{g}") for g in range(KV)]
        s_wq = [sem(f"s_wq{i}") for i in range(QPARTS)]
        s_wk = [sem(f"s_wk{k}") for k in range(KC)]
        s_ctx = [sem(f"s_ctx{k}") for k in range(KC)]
        s_wqb, s_wr, s_wrb, s_wvn, s_wf = (sem(n) for n in ("s_wqb", "s_wr", "s_wrb", "s_wvn", "s_wf"))
        s_wo = [sem(f"s_wo{i}") for i in range(4)]
        s_link = sem("s_link")
        s_zeroed = sem("s_zeroed")
        s_wk_split, s_wv_split = sem("s_wk_split"), sem("s_wv_split")
        s_wv_high = sem("s_wv_high")
        s_var, s_sd = sem("s_var"), sem("s_sd")
        s_xn = sem("s_xn")
        s_xn_turned, s_xnT, s_xnT_low = sem("s_xn_turned"), sem("s_xnT"), sem("s_xnT_low")
        s_wq_high, s_wq_low = sem("s_wq_high"), sem("s_wq_low")
        s_lat_units, s_lat_out = sem("s_lat_units"), sem("s_lat_out")
        s_klst_low = sem("s_klst_low")
        s_klat, s_vlat, s_qT = sem("s_klat"), sem("s_vlat"), sem("s_qT")
        s_ctx_high, s_ctx_low = sem("s_ctx_high"), sem("s_ctx_low")
        s_projected = sem("s_projected")
        s_k_high = sem("s_k_high")
        s_k_out, s_v_out = sem("s_k_out"), sem("s_v_out")
        s_keys, s_values_lat = sem("s_keys"), sem("s_values_lat")
        s_q_high, s_q_low = sem("s_q_high"), sem("s_q_low")
        s_scores, s_negmax, s_exps, s_probs, s_turned, s_probsT, s_probsT_lat, s_attended, s_placed = (
            sem(n) for n in ("s_scores", "s_negmax", "s_exps", "s_probs", "s_turned", "s_probsT", "s_probsT_lat",
                             "s_attended", "s_placed"))
        s_wox_high, s_wox_low, s_out_split, s_wox_done = (
            sem(n) for n in ("s_wox_high", "s_wox_low", "s_out_split", "s_wox_done"))
        s_product = sem("s_product")
        s_residual = sem("s_residual")
        s_absorbed, s_absorbed_high, s_absorbed_low = (
            sem(n) for n in ("s_absorbed", "s_absorbed_high", "s_absorbed_low"))
        s_rope_high, s_rope_low = sem("s_rope_high"), sem("s_rope_low")
        s_latents, s_squares, s_normed = sem("s_latents"), sem("s_squares"), sem("s_normed")
        s_latT, s_latT_high, s_latT_low = sem("s_latT"), sem("s_latT_high"), sem("s_latT_low")
        s_blockdiag = sem("s_blockdiag")
        s_queries, s_query_copies, s_rope_cos, s_rope_partner, s_rope_sum = (
            sem(n) for n in ("s_queries", "s_query_copies", "s_rope_cos", "s_rope_partner", "s_rope_sum"))
        s_mla_scores, s_mla_max, s_mla_shifted, s_mla_exps, s_mla_inverse, s_mla_probs, s_mla_turned, s_mla_probsT = (
            sem(n) for n in ("s_mla_scores", "s_mla_max", "s_mla_shifted", "s_mla_exps", "s_mla_inverse",
                             "s_mla_probs", "s_mla_turned", "s_mla_probsT"))
        s_weighted, s_weighted_high, s_weighted_low = (
            sem(n) for n in ("s_weighted", "s_weighted_high", "s_weighted_low"))
        s_combined, s_combined_high, s_combined_low = (
            sem(n) for n in ("s_combined", "s_combined_high", "s_combined_low"))
        s_wf_exact = sem("s_wf_exact")
        s_out = sem("s_out")

        mv = small[:, 0:4].rearrange("p (t c) -> p t c", t=TT)
        bns = small[:, 4:16].rearrange("p (t c) -> p t c", t=TT)
        va, sd, rr, nt = (small[:, 16 + 4 * i:20 + 4 * i] for i in range(4))
        mx, nm, rs, ri = (small[:, 32 + 4 * i:36 + 4 * i] for i in range(4))
        ssq = small[:, 48:52]
        mmx = [small[:, 64 + 16 * w:80 + 16 * w] for w in range(4)]
        msum = [small[:, 128 + 16 * w:144 + 16 * w] for w in range(4)]

        block = ctx.enter_context(nc.Block())

        NPRO = NK + H * HD // P + TT
        QTILES = H * HD // P

        def cbank(p):
            return p % 2 if p >= 8 else 5 if p >= 6 else 4 + p % 2

        def pieces(n):
            made = []
            pair, half = WEIGHTED[n]
            for v in range(2):
                for odd in range(2):
                    b, first = 2 * pair + v, 8 * half
                    src = ps[KL * v:KL * v + KL, B_S + n % 4, :].rearrange(
                        "p (a o s) -> p a o s", o=2, s=S)[:, :, odd, :]
                    made.append((src, lambda x, r=slice(KL * odd, KL * odd + KL), a=slice(first, first + 8),
                                 c=slice(S * b, S * b + S): x[r, a, c]))
            return made

        def kbank(b, par, j):
            return B_PROJ + (j if is_first(b) else (par + j) % 2)

        OPIECES = 1 + OG
        def vbank(b, par, i):
            return B_S + 1 if is_first(b) and i == 0 else B_PROJ + (par + NK + i) % 2

        def cuts_of(b):
            if is_first(b):
                return [4, 7, 10, 13, 16, 19, 22, 25, 28]
            if left(b) == 1:
                return [0, 4, 7, 10, 13, 16, 19, 22, 24]
            return [0, 4, 7, 11, 14, 18, 21, 25, 28]

        def values_done(b, slot):
            cuts = cuts_of(b)
            return [i for i in range(NV) if cuts[slot] < KC * (NK + i + 1) <= cuts[slot + 1]]

        KDMA = 16 * 8

        @block.sync
        def _(sp):
            for k in range(KC):
                sp.dma_start(wst[:, 0, k, :], A["wkT"][:, k, :]).then_inc(s_wk[k], 16)
                sp.dma_start(raw[:, k, :], A["ctxT"][0][:, k, :]).then_inc(s_ctx[k], 16)
            sp.dma_start(wst[:, 1], A["wvT"]).then_inc(s_wv, 16)
            sp.dma_start(xs[:], A["x"].rearrange("(t p) d -> p t d", p=P)).then_inc(s_x, 16)
            for i in range(QPARTS):
                c = slice(512 * i, 512 * i + 512)
                sp.dma_start(wq[:, :, c], A["wqT"][:, :, c]).then_inc(s_wq[i], 16)

            def context(b):
                sp.wait_ge(s_ctx_low, KC * b)
                for k in range(KC):
                    sp.dma_start(raw[:, k, :], A["ctxT"][b][:, k, :]).then_inc(s_ctx[k], 16)

            def keys(b, par):
                for j in range(NK):
                    sp.wait_ge(s_k_out, NK * b + j + 1)
                    for r, g, at, n in blocks_of(j):
                        sp.dma_start(bits(kt[par][at:at + n, :, g, 0:CTX]),
                                     bits(kst[r:r + n, :, j, :])).then_inc(s_keys, 16)

            def latents(b, par):
                for half in range(2):
                    sp.dma_start(bits(kt[par][:, half, :, CTX:KEYS]),
                                 bits(klat[:, half, :, bass.ds(S * b, S)])).then_inc(s_keys, 16)
                if is_first(b):
                    sp.wait_ge(s_vlat, 16 * TT)
                sp.dma_start(vv[par][0:S, NV, :], vlat[bass.ds(S * b, S), :]).then_inc(s_values_lat, 16)

            keys(0, 0)
            context(1)
            for m in range(NK):
                sp.wait_ge(s_klst_low, m + 1)
                for r, g, at, n in blocks_of(m):
                    sp.dma_start(bits(klat[at:at + n, :, g, :]), bits(klst[r:r + n, :, m, :])).then_inc(s_klat, 16)
            sp.wait_ge(s_klat, 16 * 6)
            for m in range(QTILES):
                sp.wait_ge(s_lat_out, NK + m + 1)
                for r, h, at, n in blocks_of(m):
                    sp.dma_start(qT[at:at + n, h, :], qst[r:r + n, m, :]).then_inc(s_qT, 16)
            for t in range(TT):
                sp.wait_ge(s_lat_out, NK + QTILES + t + 1)
                sp.dma_start(vlat[P * t:P * t + P, :], vlst[:, t, :]).then_inc(s_vlat, 16)
            latents(0, 0)
            context(2)

            def out_weights(g):
                sp.dma_start(wox[g][:], A["woxT"][:, OG * g:OG * g + OG, :]).then_inc(s_wox[g], 16)

            def follow(b, par):
                if left(b) >= 1:
                    if not is_first(b):
                        sp.wait_ge(s_scores, KV * b)
                        sp.wait_ge(s_attended, KV * b)
                    keys(b + 1, 1 - par)
                    latents(b + 1, 1 - par)
                if left(b) >= 3:
                    context(b + 3)
                if left(b) == 2:
                    sp.wait_ge(s_ctx_low, KC * B)
                    out_weights(0)
                if left(b) == 1:
                    sp.wait_ge(s_q_low, B)
                    out_weights(2)
                    out_weights(3)

            each_batch(sp, follow)

            sp.wait_ge(s_projected, NU * B)
            sp.wait_ge(s_wox_low, OG)
            out_weights(1)
            sp.dma_start(wqb[:], A["wqbn"]).then_inc(s_wqb, 16)
            sp.wait_ge(s_wox_low, 2 * OG)
            sp.dma_start(wkn[:], A["wkn"]).then_inc(s_wqb, 16)
            sp.wait_ge(s_attended, KV * B)
            sp.dma_start(wrb[:], A["wqrb"]).then_inc(s_wrb, 16)
            sp.dma_start(wra[:], A["wqra"]).then_inc(s_wr, 16)
            sp.dma_start(wa[:], A["waT"]).then_inc(s_wr, 16)
            sp.wait_ge(s_out_split, KV)
            sp.dma_start(wo0[:], A["wob"][:, 0:8, :]).then_inc(s_wo[0], 16)
            sp.dma_start(wo1[:], A["wob"][:, 8:16, :]).then_inc(s_wo[1], 16)
            sp.wait_ge(s_absorbed, 4)
            sp.dma_start(wvn[:], A["wvn"]).then_inc(s_wvn, 16)
            sp.dma_start(wo2[:], A["wob"][:, 16:24, :]).then_inc(s_wo[2], 16)
            sp.wait_ge(s_latents, TT)
            sp.wait_ge(s_rope_low, 2)
            sp.dma_start(wo3[:], A["wob"][:, 24:32, :]).then_inc(s_wo[3], 16)
            sp.wait_ge(s_queries, NH // 2)
            sp.dma_start(wf16[:], A["wfT"]).then_inc(s_wf, 16)
            for t in range(TT):
                sp.wait_ge(s_residual, 2 * TT + t + 1)
                sp.dma_start(out[P * t:P * t + P, :], xs[:, t, :]).then_inc(s_out, 16)
            sp.wait_ge(s_out, 16 * TT)

        @block.gpsimd
        def _(pool):
            def low(b, par, k):
                pool.wait_ge(s_ctx_high, KC * b + k + 1)
                pool.tensor_tensor(hl[par][:, k, :], raw[:, k, :], hh[par][:, k, :],
                                   ALU.subtract).then_inc(s_ctx_low, 1)

            def queries(b, par):
                pool.tensor_copy(qc[par][:, 0], qT[:, :, bass.ds(b * S, S)]).then_inc(s_q_high, 1)

            def wox_low(g):
                for i in range(OG):
                    pool.wait_ge(s_wox_high, OG * g + i + 1)
                    pool.tensor_tensor(hl[g % 2][:, i, :], wox[g][:, i, :], hh[g % 2][:, i, :],
                                       ALU.subtract).then_inc(s_wox_low, 1)

            pool.memset(bd[:], 0.0).then_inc(s_zeroed, 1)
            for k in range(KC):
                low(0, 0, k)
            for k in range(KC):
                pool.wait_ge(s_wv_high, k + 1)
                pool.tensor_tensor(wvl[:, k, :], wst[:, 1, k, :], wvh[:, k, :], ALU.subtract).then_inc(s_wv_split, 1)
            for m in range(QTILES):
                c = slice(P * (m % 4), P * (m % 4) + P)
                pool.wait_ge(s_wq_high, m + 1)
                pool.tensor_tensor(hl1[:, :, c], wq[:, :, P * m:P * m + P], hh1[:, :, c],
                                   ALU.subtract).then_inc(s_wq_low, 1)
            pool.wait_ge(s_q_high, 1)
            def ahead_of(b, par):
                if left(b) >= 1:
                    if not is_first(b):
                        pool.wait_ge(s_scores, KV * b)
                    queries(b + 1, 1 - par)
                if left(b) >= 2:
                    for k in range(KC):
                        low(b + 2, par, k)

            each_batch(pool, ahead_of)
            for g in range(KV):
                wox_low(g)

            pool.wait_ge(s_wox_low, OT)
            pool.wait_ge(s_rope_high, 1)
            pool.tensor_tensor(wqps[QB:P, :, KL:P], wrb[:], wqps[0:QB, :, KL:P], ALU.subtract).then_inc(s_rope_low, 1)
            pool.wait_ge(s_rope_high, 2)
            pool.wait_ge(s_rope_low, 1)
            pool.tensor_tensor(wqpl[:, :, KL:P], wra[:], wqph[:, :, KL:P], ALU.subtract).then_inc(s_rope_low, 1)

            def rope_add(lo, hi):
                for n in range(lo, hi):
                    if n % 2 == 0:
                        pool.wait_ge(s_query_copies, 3 * (n // 2) + 1)
                        if n >= 2:
                            pool.wait_ge(s_rope_sum, n)
                        down = ropeq[KL:KL + 32, 1:2, :].to_broadcast([32, 2 * B, S])
                        pool.tensor_tensor(t2[KL + 32:P, 0, :].rearrange("p (a s) -> p a s", s=S),
                                           rope_raw[KL:KL + 32, :].rearrange("p (a s) -> p a s", s=S),
                                           down, ALU.mult).then_inc(s_rope_partner, 1)
                        pool.wait_ge(s_rope_partner, n // 2 + 1)
                    pool.wait_ge(s_rope_cos, n + 1)
                    rows = qp[KL:P, :, 2 * n:2 * n + 2, :]
                    part = t2[KL:P, n % 2, :].rearrange("p (h b s) -> p b h s", h=2, s=S)
                    pool.tensor_tensor(rows, rows, part, ALU.add).then_inc(s_rope_sum, 1)

            def stat(tile):
                return tile.unsqueeze(2).to_broadcast([P, 16, 32])

            def shift(w):
                sc = pm[:, w, :].rearrange("p (a t) -> p a t", a=16)
                pool.wait_ge(s_mla_max, w + 1)
                pool.tensor_tensor(sc, sc, stat(mmx[w]), ALU.subtract).then_inc(s_mla_shifted, 1)

            def norm(w):
                sc = pm[:, w, :].rearrange("p (a t) -> p a t", a=16)
                pool.wait_ge(s_mla_inverse, w + 1)
                pool.tensor_tensor(sc, sc, stat(msum[w]), ALU.mult).then_inc(s_mla_probs, 1)

            pool.wait_ge(s_rope_low, 2)
            rope_add(0, 8)
            pool.wait_ge(s_rope_sum, 8)
            shift(0)
            pool.wait_ge(s_mla_shifted, 1)
            rope_add(8, 12)
            pool.wait_ge(s_rope_sum, 12)
            norm(0)
            shift(1)
            pool.wait_ge(s_mla_probs, 1)
            pool.wait_ge(s_mla_shifted, 2)
            rope_add(12, 16)
            pool.wait_ge(s_rope_sum, 16)
            norm(1)

        @block.scalar
        def _(act):
            act.wait_ge(s_ctx[KC - 1], 16)
            act.dma_start(ident[:], A["ident"]).then_inc(s_const, 16)
            act.dma_start(ropek[:], A["ropek"]).then_inc(s_const, 16)
            act.dma_start(ropeq[:], A["ropeq"]).then_inc(s_const, 16)
            act.dma_start(cap[:], A["cap"]).then_inc(s_const, 16)
            act.dma_start(qnw[:], A["qnw"].partition_broadcast(P)).then_inc(s_const, 16)
            act.dma_start(kvnw[:], A["kvnw"].partition_broadcast(P)).then_inc(s_const, 16)
            act.dma_start(bias[:], A["bias"].partition_broadcast(P)).then_inc(s_const, 16)

            def root(n, lo, hi):
                act.wait_ge(s_var, n)
                act.activation(sd[:, lo:hi], va[:, lo:hi], ACT.Sqrt).then_inc(s_sd, 1)

            def turn_out(n, bank, dst, first=0, last=TT):
                for t in range(first, last):
                    act.wait_ge(s_xn_turned, TT * n + t + 1)
                    act.copy(dst[:, :, P * t:P * t + P],
                             ps[:, bank + t, :].rearrange("p (k c) -> p k c", k=KC)).then_inc(s_xnT, 1)

            def v_out(b, par, i):
                n = NU * b + NK + i
                act.wait_ge(s_projected, n + 1)
                act.copy(vv[par][:, i, :], ps[:, vbank(b, par, i), 0:KVD]).then_inc(s_v_out, 1)

            for j in range(NK):
                act.wait_ge(s_projected, j + 1)
                act.copy(kst[:, 0, j, :], ps[:, kbank(0, 0, j), :]).then_inc(s_k_high, 1)
            root(1, 0, TT)
            for i in range(NV - 1):
                v_out(0, 0, i)
            turn_out(0, B_S, xh)
            v_out(0, 0, NV - 1)
            for m in range(NPRO):
                act.wait_ge(s_lat_units, m + 1)
                bank = ps[:, B_PT + m % 4, :]
                if m < NK:
                    dst, src = klst[:, 0, m, :], bank[:, 0:TOK]
                elif m < NK + QTILES:
                    dst, src = qst[:, m - NK, :], bank[:, 0:TOK]
                else:
                    dst, src = vlst[:, m - NK - QTILES, :], bank[:, 0:KVD]
                act.copy(dst, src).then_inc(s_lat_out, 1)

            def softmax(b, par):
                more = left(b) >= 1
                for g in range(KV):
                    n = KV * b + g
                    fresh = is_first(b) and g == 0
                    act.wait_ge(s_negmax, n + 1)
                    if not fresh:
                        act.wait_ge(s_turned, n)
                    act.activation(pr[:].rearrange("p (a k) -> p a k", a=2), ps[:, B_S:B_S + 2, 0:HALF], ACT.Exp,
                                   bias=nm[:, g:g + 1], scale=XSCALE, accum_out=rs[:, g:g + 1]).then_inc(s_exps, 1)
                    if more:
                        for i in values_done(b, 2 * g):
                            v_out(b + 1, 1 - par, i)
                    act.wait_ge(s_turned, n + 1)
                    if not fresh:
                        act.wait_ge(s_attended, n)
                    act.copy(pt[:], ps[:, B_PT, :]).then_inc(s_probsT, 1)
                    if more:
                        for i in values_done(b, 2 * g + 1):
                            v_out(b + 1, 1 - par, i)
                    elif g == 0:
                        v_out(b, par, NV - 1)

            each_batch(act, softmax)

            act.wait_ge(s_wrb, 16)
            act.wait_ge(s_wox_low, OT)
            act.copy(wqps[0:QB, :, KL:P], wrb[:]).then_inc(s_rope_high, 1)
            root(2, 0, TT)

            def absorbed_high(m):
                bank = B_S if m % 2 == 0 else B_O
                act.wait_ge(s_absorbed, m + 1)
                act.copy(wqph[:, 8 * m:8 * m + 8, 0:KL],
                         ps[:, bank, :].rearrange("p (h c) -> p h c", h=8)).then_inc(s_absorbed_high, 1)
                act.copy(wqps[0:QB, 8 * m:8 * m + 8, 0:KL],
                         ps[0:QB, bank + 1, :].rearrange("p (h c) -> p h c", h=8)).then_inc(s_absorbed_high, 1)

            act.wait_ge(s_product, TT)
            act.wait_ge(s_wr, 32)
            act.copy(wqph[:, :, KL:P], wra[:]).then_inc(s_rope_high, 1)
            absorbed_high(0)
            turn_out(1, B_PROJ, xnT)
            absorbed_high(1)
            for t in range(TT):
                act.wait_ge(s_latents, t + 1)
                act.activation(xn[:, t, 0:QL], ps[:, B_PT + t, 0:QL], ACT.Square,
                               accum_out=ssq[:, t:t + 1]).then_inc(s_squares, 1)
                act.activation(xn[:, t, QL:QL + KL], ps[:, B_PT + t, QL:QL + KL], ACT.Square,
                               accum_out=ssq[:, TT + t:TT + t + 1]).then_inc(s_squares, 1)
            root(3, 0, 2 * TT)
            absorbed_high(2)
            act.wait_ge(s_latT, 1)
            act.copy(qlah[:], ps[:, B_PROJ, 0:TOK]).then_inc(s_latT_high, 1)
            act.copy(qlbh[0:QB], ps[0:QB, B_PROJ, TOK:2 * TOK]).then_inc(s_latT_high, 1)
            act.wait_ge(s_latT_high, 2)
            act.copy(qlbh[QB:P], qlbh[0:QB]).then_inc(s_latT_high, 1)
            absorbed_high(3)
            act.wait_ge(s_latT, 2)
            act.copy(kpT[:], ps[:, B_PROJ + 1, 0:TOK]).then_inc(s_latT_high, 1)

            def absorbed_out(lo, hi):
                for n in range(lo, hi):
                    act.wait_ge(s_queries, n + 1)
                    if n % 2 == 0:
                        if n >= 2:
                            act.wait_ge(s_rope_partner, n // 2)
                        act.copy(rope_raw[KL:KL + 32, :], ps[KL:KL + 32, QBANK[n % 4], :]).then_inc(s_query_copies, 1)
                    act.copy(qp[0:KL, :, 2 * n:2 * n + 2, :],
                             ps[0:KL, QBANK[n % 4], :].rearrange(
                                 "p (h b s) -> p b h s", h=2, s=S)).then_inc(s_query_copies, 1)

            def exps(w):
                act.wait_ge(s_mla_shifted, w + 1)
                act.activation(pm[:, w, :], pm[:, w, :], ACT.Exp, scale=MSCALE).then_inc(s_mla_exps, 1)

            def combined_high(p):
                act.wait_ge(s_combined, p + 1)
                act.copy(wc[p // 4][:, 2 * (p % 4), :], ps[:, cbank(p), :]).then_inc(s_combined_high, 1)

            def weighted_high(n):
                act.wait_ge(s_weighted, n + 1)
                for src, at in pieces(n):
                    act.copy(at(och), src).then_inc(s_weighted_high, 1)

            def scores_out(w):
                act.wait_ge(s_mla_turned, w + 1)
                act.copy(ptm[:, :, 2 * w:2 * w + 2, :],
                         ps[:, B_O + w % 2, :].rearrange("p (t g c) -> p t g c", t=TT, g=2)).then_inc(s_mla_probsT, 1)

            absorbed_out(0, 4)
            combined_high(0)
            absorbed_out(4, 6)
            combined_high(1)
            combined_high(2)
            absorbed_out(6, 8)
            combined_high(3)
            for p in (4, 5):
                absorbed_out(2 * p, 2 * p + 2)
                combined_high(p)
            exps(0)
            for p in (6, 7):
                absorbed_out(2 * p, 2 * p + 2)
                combined_high(p)
            combined_high(8)
            exps(1)
            combined_high(9)
            combined_high(10)
            exps(2)
            scores_out(0)
            scores_out(1)
            exps(3)
            combined_high(11)
            weighted_high(0)
            weighted_high(1)
            combined_high(12)
            scores_out(2)
            combined_high(13)
            scores_out(3)
            weighted_high(2)
            weighted_high(3)
            combined_high(14)
            combined_high(15)
            for n in range(4, 8):
                weighted_high(n)
            for t in range(TT):
                root(4 + t, t, t + 1)
                turn_out(2, B_PROJ, x3h, t, t + 1)

        @block.vector
        def _(dve):
            chain = [0, 0]

            def link(ins):
                chain[0] += 1
                ins.then_inc(s_link, 1)
                dve.wait_ge(s_link, chain[0] + chain[1])

            def inverse_root(n, lo, hi):
                dve.wait_ge(s_sd, n)
                link(dve.reciprocal(rr[:, lo:hi], sd[:, lo:hi]))
                link(dve.tensor_tensor(nt[:, lo:hi], rr[:, lo:hi], rr[:, lo:hi], ALU.mult))
                link(dve.tensor_tensor(nt[:, lo:hi], nt[:, lo:hi], va[:, lo:hi], ALU.mult))
                link(dve.tensor_scalar(nt[:, lo:hi], nt[:, lo:hi], -0.5, 1.5, ALU.mult, ALU.add))
                link(dve.tensor_tensor(rr[:, lo:hi], rr[:, lo:hi], nt[:, lo:hi], ALU.mult))

            def stats(t):
                link(dve.bn_stats(bns[:, t, :], xs[:, t, :]))
                link(dve.bn_aggr(mv[:, t, :], bns[:, t, :]))

            def normalise(n, lo, hi):
                dve.tensor_scalar(va[:, lo:hi], mv[:, lo:hi, 1], LN_EPS, None, ALU.add).then_inc(s_var, 1)
                inverse_root(n, lo, hi)
                for t in range(lo, hi):
                    dve.tensor_scalar(xn[:, t, :], xs[:, t, :], mv[:, t, 0:1], rr[:, t:t + 1],
                                      ALU.subtract, ALU.mult).then_inc(s_xn, 1)

            def high(b, par, k):
                dve.wait_ge(s_ctx[k], 16 * (b + 1))
                dve.tensor_copy(hh[par][:, k, :], raw[:, k, :]).then_inc(s_ctx_high, 1)

            def turn_low(n, bank, hi, lo, first=0, last=TT):
                for t in range(first, last):
                    c = slice(P * t, P * t + P)
                    dve.wait_ge(s_xnT, TT * n + t + 1)
                    dve.tensor_tensor(lo[:, :, c], ps[:, bank + t, :].rearrange("p (k c) -> p k c", k=KC), hi[:, :, c],
                                      ALU.subtract).then_inc(s_xnT_low, 1)

            def k_out(b, par, j):
                dve.wait_ge(s_projected, NU * b + j + 1)
                bank = ps[:, kbank(b, par, j), :]
                if not is_first(b):
                    dve.tensor_copy(kst[:, 0, j, :], bank).then_inc(s_k_high, 1)
                dve.wait_ge(s_k_high, NK * b + j + 1)
                dve.tensor_tensor(kst[:, 1, j, :], bank, kst[:, 0, j, :], ALU.subtract).then_inc(s_k_out, 1)

            for k in range(KC):
                dve.wait_ge(s_wk[k], 16)
                link(dve.tensor_copy(wkh[:, k, :], wst[:, 0, k, :]))
                dve.tensor_tensor(wkl[:, k, :], wst[:, 0, k, :], wkh[:, k, :], ALU.subtract).then_inc(s_wk_split, 1)
                high(0, 0, k)
            dve.wait_ge(s_wv, 16)

            def wv_high(k):
                dve.tensor_copy(wvh[:, k, :], wst[:, 1, k, :]).then_inc(s_wv_high, 1)

            for k in range(KC):
                wv_high(k)
            for j in range(NK):
                k_out(0, 0, j)
            dve.wait_ge(s_x, 16)
            for t in range(TT):
                stats(t)
            normalise(1, 0, TT)

            def wq_high(m):
                if m >= 4:
                    dve.wait_ge(s_lat_units, NK + m - 3)
                if m % 4 == 0:
                    dve.wait_ge(s_wq[m // 4], 16)
                c = slice(P * (m % 4), P * (m % 4) + P)
                dve.tensor_copy(hh1[:, :, c], wq[:, :, P * m:P * m + P]).then_inc(s_wq_high, 1)

            for m in range(4):
                wq_high(m)
            turn_low(0, B_S, xh, xl)
            for m in range(NK):
                dve.wait_ge(s_lat_out, m + 1)
                dve.tensor_tensor(klst[:, 1, m, :], ps[:, B_PT + m % 4, 0:TOK], klst[:, 0, m, :],
                                  ALU.subtract).then_inc(s_klst_low, 1)
            for m in range(4, QTILES):
                wq_high(m)
            dve.wait_ge(s_lat_units, NK + QTILES)
            for k in range(KC):
                high(1, 1, k)
                dve.wait_ge(s_ctx_high, KC + k + 1)
                dve.tensor_tensor(hl1[:, k, :], raw[:, k, :], hh1[:, k, :], ALU.subtract).then_inc(s_ctx_low, 1)

            dve.wait_ge(s_qT, 16 * 24)
            dve.tensor_copy(qc[0][:, 0], qT[:, :, 0:S]).then_inc(s_q_high, 1)

            def query_low(b, par):
                dve.wait_ge(s_q_high, b + 1)
                dve.tensor_tensor(qc[par][:, 1], qT[:, :, bass.ds(b * S, S)], qc[par][:, 0], ALU.subtract
                                  ).then_inc(s_q_low, 1)

            query_low(0, 0)

            def o_out(b, g):
                dve.wait_ge(s_attended, KV * b + g + 1)
                o, c = ps[:, B_O + g % 2, 0:P], bass.ds(S * b, S)
                dve.tensor_copy(outT[0:HD, OG * g:OG * g + OG, c],
                                o[0:HD, 0:OG * S].rearrange("p (h s) -> p h s", h=OG)).then_inc(s_placed, 1)
                for i in range(OG):
                    dve.tensor_copy(outT[HD:P, OG * g + i, c], o[32 * i:32 * i + 32, OG * S:P]).then_inc(s_placed, 1)

            def o_split(g):
                dve.wait_ge(s_placed, OPIECES * (KV * (B - 1) + g + 1))
                if g >= 2:
                    dve.wait_ge(s_wox_done, g - 1)
                link(dve.tensor_copy(oh[:, g % 2], outT[:, OG * g:OG * g + OG, :]))
                dve.tensor_tensor(ol[:, g % 2], outT[:, OG * g:OG * g + OG, :], oh[:, g % 2], ALU.subtract
                                  ).then_inc(s_out_split, 1)

            def wox_high(g, i):
                if i == 0:
                    dve.wait_ge(s_wox[g], 16)
                dve.tensor_copy(hh[g % 2][:, i, :], wox[g][:, i, :]).then_inc(s_wox_high, 1)

            def batch(b, par):
                more, ahead, last = left(b) >= 1, left(b) >= 2, left(b) == 0
                for g in range(KV):
                    n = KV * b + g
                    dve.wait_ge(s_scores, n + 1)
                    link(dve.tensor_reduce(mx[:, g:g + 1], ps[:, B_S:B_S + 2, 0:HALF], AX.XY, ALU.max))
                    dve.tensor_scalar(nm[:, g:g + 1], mx[:, g:g + 1], -XSCALE, None, ALU.mult).then_inc(s_negmax, 1)
                    if g > 0:
                        o_out(b, g - 1)
                    elif not is_first(b):
                        o_out(b - 1, KV - 1)
                    if more and g == 1:
                        k_out(b + 1, 1 - par, 1)
                    dve.wait_ge(s_exps, n + 1)
                    link(dve.reciprocal(ri[:, g:g + 1], rs[:, g:g + 1]))
                    dve.tensor_scalar(pr[:], pr[:], ri[:, g:g + 1], None, ALU.mult).then_inc(s_probs, 1)
                    if more and g == 0:
                        dve.wait_ge(s_keys, KDMA * (b + 1))
                        k_out(b + 1, 1 - par, 0)
                    if ahead:
                        if g == 0:
                            dve.wait_ge(s_projected, NU * (b + 1))
                        high(b + 2, par, g)
                    elif not last:
                        if g == 0:
                            dve.wait_ge(s_projected, NU * (B - 1))
                        if g < OG:
                            wox_high(0, g)
                    dve.wait_ge(s_turned, n + 1)
                    dve.tensor_copy(pt4[:], ps[0:S, B_PT + 1, 0:P]).then_inc(s_probsT_lat, 1)
                    if last and g > 0:
                        o_split(g - 1)
                    if more and g == 1:
                        k_out(b + 1, 1 - par, 2)
                    if more and g == 2:
                        query_low(b + 1, 1 - par)
                    if last:
                        if g == 1:
                            dve.wait_ge(s_projected, NU * B)
                        if g >= 2:
                            dve.wait_ge(s_wox_done, g - 1)
                        if g > 0:
                            for i in range(OG):
                                wox_high(g, i)
            batch(0, 0)
            links = 2 * 2 * KV
            with dve.Fori(0, PAIRS) as i:
                before, chain[1] = chain[0], links * i
                for u in (1, 2):
                    batch(2 * i + u, u % 2)
                assert chain[0] == before + links
            chain[:] = [before + links * PAIRS, 0]
            for b in range(2 * PAIRS + 1, B):
                batch(b, b % 2)
            o_out(B - 1, KV - 1)
            o_split(KV - 1)

            for t in range(TT):
                dve.wait_ge(s_product, t + 1)
                dve.tensor_tensor(xs[:, t, :], xs[:, t, :], ps[:, B_PROJ + t, :], ALU.add).then_inc(s_residual, 1)
                dve.wait_ge(s_residual, t + 1)
                stats(t)
            normalise(2, 0, TT)

            def absorbed_low(m):
                bank = B_S if m % 2 == 0 else B_O
                r = slice(8 * m, 8 * m + 8)
                dve.wait_ge(s_absorbed_high, 2 * m + 2)
                dve.tensor_tensor(wqpl[:, r, 0:KL], ps[:, bank, :].rearrange("p (h c) -> p h c", h=8),
                                  wqph[:, r, 0:KL], ALU.subtract).then_inc(s_absorbed_low, 1)
                dve.tensor_tensor(wqps[QB:P, r, 0:KL], ps[0:QB, bank + 1, :].rearrange("p (h c) -> p h c", h=8),
                                  wqps[0:QB, r, 0:KL], ALU.subtract).then_inc(s_absorbed_low, 1)

            for m in range(2):
                absorbed_low(m)
            dve.wait_ge(s_squares, 2 * TT)
            link(dve.tensor_scalar(va[:, 0:TT], ssq[:, 0:TT], 1.0 / QL, RMS_EPS, ALU.mult, ALU.add))
            dve.tensor_scalar(va[:, TT:2 * TT], ssq[:, TT:2 * TT], 1.0 / KL, RMS_EPS,
                              ALU.mult, ALU.add).then_inc(s_var, 1)
            inverse_root(3, 0, 2 * TT)
            for t in range(TT):
                lat = ps[:, B_PT + t, :]
                dve.scalar_tensor_tensor(out=ql[:, t, :], in0=lat[:, 0:QL], scalar=rr[:, t:t + 1], in1=qnw[:],
                                         op0=ALU.mult, op1=ALU.mult).then_inc(s_normed, 1)
            for t in range(TT):
                lat = ps[:, B_PT + t, :]
                link(dve.scalar_tensor_tensor(out=kp[:, t, 0:KL], in0=lat[:, QL:QL + KL],
                                              scalar=rr[:, TT + t:TT + t + 1], in1=kvnw[:],
                                              op0=ALU.mult, op1=ALU.mult))
            x1 = ps[:, B_PT:B_PT + TT, QL + KL:QL + KL + 32]
            x2 = ps[:, B_PT:B_PT + TT, QL + KL + 32:LAT]
            cos, sin = (ropek[:, i:i + 1, :].to_broadcast([P, TT, 32]) for i in range(2))
            rot = xn[:, 0, 256:512].rearrange("p (a t c) -> p a t c", a=4, t=TT)
            for i, (a, w) in enumerate(((x1, cos), (x2, sin), (x1, sin), (x2, cos))):
                link(dve.tensor_tensor(rot[:, i], a, w, ALU.mult))
            dve.tensor_tensor(kp[:, :, KL:KL + 32], rot[:, 0], rot[:, 1], ALU.subtract).then_inc(s_normed, 1)
            dve.tensor_tensor(kp[:, :, KL + 32:P], rot[:, 2], rot[:, 3], ALU.add).then_inc(s_normed, 1)
            dve.wait_ge(s_latT_high, 2)
            dve.tensor_tensor(qlal[:], ps[:, B_PROJ, 0:TOK], qlah[:], ALU.subtract).then_inc(s_latT_low, 1)
            dve.tensor_tensor(qlbl[:], ps[0:QB, B_PROJ, TOK:2 * TOK], qlbh[0:QB], ALU.subtract).then_inc(s_latT_low, 1)

            absorbed_low(2)
            absorbed_low(3)

            def rope(lo, hi):
                for n in range(lo, hi):
                    dve.wait_ge(s_queries, n + 1)
                    if n >= 2:
                        dve.wait_ge(s_rope_sum, n - 1)
                    q = ps[:, QBANK[n % 4], :].rearrange("p (a s) -> p a s", s=S)
                    qb = ps[:, QBANK[n % 4], :].rearrange("p (h b s) -> p b h s", h=2, s=S)
                    tt = t2[:, n % 2, :].rearrange("p (a s) -> p a s", s=S)
                    cosb = ropeq[KL:P, 0:1, :].unsqueeze(1).to_broadcast([P - KL, B, 2, S])
                    up, down = (ropeq[r:r + 32, 1:2, :].to_broadcast([32, 2 * B, S]) for r in (KL + 32, KL))
                    dve.tensor_tensor(tt[KL:KL + 32], q[KL + 32:P], up, ALU.mult).then_inc(s_link, 1)
                    chain[0] += 1
                    if n % 2:
                        dve.tensor_tensor(tt[KL + 32:P], q[KL:KL + 32], down, ALU.mult).then_inc(s_link, 1)
                        chain[0] += 1
                    else:
                        dve.wait_ge(s_query_copies, 3 * (n // 2) + 1)
                    dve.tensor_tensor(qp[KL:P, :, 2 * n:2 * n + 2, :], qb[KL:P], cosb, ALU.mult).then_inc(s_rope_cos, 1)

            capb = cap[:].unsqueeze(1).to_broadcast([P, 16, 32])

            def largest(w):
                sc = pm[:, w, :].rearrange("p (a t) -> p a t", a=16)
                dve.wait_ge(s_mla_scores, w + 1)
                link(dve.tensor_tensor(sc, ps[:, B_S + w, :].rearrange("p (a t) -> p a t", a=16), capb, ALU.min))
                dve.tensor_reduce(mmx[w], sc, AX.X, ALU.max).then_inc(s_mla_max, 1)

            def total(w):
                dve.wait_ge(s_mla_exps, w + 1)
                link(dve.tensor_reduce(msum[w], pm[:, w, :].rearrange("p (a t) -> p a t", a=16), AX.X, ALU.add))
                dve.reciprocal(msum[w], msum[w]).then_inc(s_mla_inverse, 1)

            def blockdiag():
                dve.wait_ge(s_zeroed, 1)
                for u in range(4):
                    r = slice(S * u, S * u + S)
                    dve.tensor_copy(bd[r, :, u // 2, KL * (u % 2):KL * (u % 2) + KL],
                                    kp[r, :, 0:KL]).then_inc(s_blockdiag, 1)

            def shift(w):
                sc = pm[:, w, :].rearrange("p (a t) -> p a t", a=16)
                dve.wait_ge(s_mla_max, w + 1)
                dve.tensor_tensor(sc, sc, mmx[w].unsqueeze(2).to_broadcast([P, 16, 32]), ALU.subtract
                                  ).then_inc(s_mla_shifted, 1)

            def norm(w):
                sc = pm[:, w, :].rearrange("p (a t) -> p a t", a=16)
                dve.wait_ge(s_mla_inverse, w + 1)
                dve.tensor_tensor(sc, sc, msum[w].unsqueeze(2).to_broadcast([P, 16, 32]), ALU.mult
                                  ).then_inc(s_mla_probs, 1)

            def combined_low(p):
                dve.wait_ge(s_combined_high, p + 1)
                at = 2 * (p % 4)
                dve.tensor_tensor(wc[p // 4][:, at + 1, :], ps[:, cbank(p), :], wc[p // 4][:, at, :],
                                  ALU.subtract).then_inc(s_combined_low, 1)

            def weighted_low(n):
                for i, (src, at) in enumerate(pieces(n)):
                    dve.wait_ge(s_weighted_high, 4 * n + 2 * (i // 2) + 2)
                    dve.tensor_tensor(at(ocl), src, at(och), ALU.subtract).then_inc(s_weighted_low, 1)

            rope(0, 4)
            combined_low(0)
            rope(4, 6)
            combined_low(1)
            combined_low(2)
            rope(6, 8)
            combined_low(3)
            largest(0)
            for p in (4, 5):
                rope(2 * p, 2 * p + 2)
                combined_low(p)
            total(0)
            largest(1)
            for p in (6, 7):
                rope(2 * p, 2 * p + 2)
                combined_low(p)
            combined_low(8)
            largest(2)
            total(1)
            dve.wait_ge(s_mla_shifted, 2)
            shift(2)
            combined_low(9)
            blockdiag()
            largest(3)
            shift(3)
            total(2)
            dve.wait_ge(s_mla_probs, 2)
            norm(2)
            combined_low(10)
            combined_low(11)
            total(3)
            norm(3)
            weighted_low(0)
            weighted_low(1)
            combined_low(12)
            combined_low(13)
            weighted_low(2)
            weighted_low(3)
            combined_low(14)
            combined_low(15)
            for n in range(4, 8):
                weighted_low(n)
            dve.wait_ge(s_wf, 16)
            dve.tensor_copy(wf[:], wf16[:]).then_inc(s_wf_exact, 1)
            for t in range(TT):
                dve.wait_ge(s_product, TT + t + 1)
                dve.tensor_tensor(xs[:, t, :], xs[:, t, :], ps[:, B_O + t, :], ALU.add).then_inc(s_residual, 1)
                dve.wait_ge(s_residual, TT + t + 1)
                stats(t)
                dve.tensor_scalar(xn[:, t, :], xs[:, t, :], mv[:, t, 0:1], None, ALU.subtract).then_inc(s_xn, 1)
                dve.tensor_scalar(va[:, t:t + 1], mv[:, t:t + 1, 1], LN_EPS, None, ALU.add).then_inc(s_var, 1)
                inverse_root(4 + t, t, t + 1)
                turn_low(2, B_PROJ, x3h, x3l, t, t + 1)
                link(dve.tensor_tensor(xs[:, t, :], xs[:, t, :], bias[:], ALU.add))
            for t in range(TT):
                dve.wait_ge(s_product, 2 * TT + t + 1)
                dve.scalar_tensor_tensor(out=xs[:, t, :], in0=ps[:, B_S + t, :], scalar=rr[:, t:t + 1],
                                         in1=xs[:, t, :], op0=ALU.mult, op1=ALU.add).then_inc(s_residual, 1)

        @block.tensor
        def _(pe):
            def three(o, stationary, moving, first, last):
                (wh, wl), (mh, ml) = stationary, moving
                for i, (w, m) in enumerate(((wh, mh), (wl, mh), (wh, ml))):
                    mm = pe.matmul(o, w, m, start=first and i == 0, stop=last and i == 2)
                return mm

            def project(b, par, first, last):
                for step in range(first, last):
                    u, k = step // KC, step % KC
                    if is_first(b) and u < NK:
                        u, k = step % NK, step // NK
                    bank = kbank(b, par, u) if u < NK else vbank(b, par, u - NK)
                    if is_first(b) and u == 0:
                        pe.wait_ge(s_ctx_low, k + 1)
                        pe.wait_ge(s_wk_split, k + 1)
                    if not is_first(b) and step < KC:
                        pe.wait_ge(s_ctx_low, KC * b + KC)
                    if is_first(b) and u == NK:
                        pe.wait_ge(s_wv_split, k + 1)
                    if k == 0:
                        if u < 2 and not is_first(b):
                            pe.wait_ge(s_v_out, NV * (b - 1) + 3 + u)
                        elif 2 <= u < NK + 2 and (u > NK or not is_first(b)):
                            pe.wait_ge(s_k_out, NK * b + u - 1)
                        elif u >= NK + 2:
                            pe.wait_ge(s_v_out, NV * b + u - NK - 1)
                    if u < NK:
                        c = slice(P * u, P * u + P)
                        mm = three(ps[:, bank, :], (wkh[:, k, c], wkl[:, k, c]),
                                   (hh[par][:, k, :], hl[par][:, k, :]), k == 0, k == KC - 1)
                    else:
                        c = slice(P * (u - NK), P * (u - NK) + P)
                        mm = three(ps[:, bank, 0:KVD], (hh[par][:, k, c], hl[par][:, k, c]),
                                   (wvh[:, k, :], wvl[:, k, :]), k == 0, k == KC - 1)
                    if k == KC - 1:
                        mm.then_inc(s_projected, 1)

            def turn(n, bank, first=0, last=TT):
                for t in range(first, last):
                    pe.wait_ge(s_xn, TT * n + t + 1)
                    for k in range(KC):
                        tr = pe.transpose(ps[:, bank + t, P * k:P * k + P], xn[:, t, P * k:P * k + P], ident[:])
                    tr.then_inc(s_xn_turned, 1)

            pe.wait_ge(s_zeroed, 1)
            for _ in range(WARM):
                pe.matmul(ps[:, B_PT, 0:TOK], bd[:, 0, 0, :], bd[:, 0].rearrange("p a c -> p (a c)"),
                          start=True, stop=True)
            project(0, 0, 0, (NU - 1) * KC)
            pe.wait_ge(s_const, 16 * 7)
            turn(0, B_S)
            project(0, 0, (NU - 1) * KC, NU * KC)
            pe.wait_ge(s_xnT_low, TT)
            for m in range(NPRO):
                if m >= 4:
                    pe.wait_ge(s_lat_out, m - 3)
                    pe.wait_ge(s_klst_low, min(m - 3, NK))
                bank = B_PT + m % 4
                for k in range(KC):
                    ends = (k == 0, k == KC - 1)
                    if m < NK:
                        c = slice(P * m, P * m + P)
                        mm = three(ps[:, bank, 0:TOK], (wkh[:, k, c], wkl[:, k, c]), (xh[:, k, :], xl[:, k, :]), *ends)
                    elif m < NK + QTILES:
                        q = m - NK
                        if k == 0:
                            pe.wait_ge(s_wq_low, q + 1)
                        c = slice(P * (q % 4), P * (q % 4) + P)
                        mm = three(ps[:, bank, 0:TOK], (hh1[:, k, c], hl1[:, k, c]), (xh[:, k, :], xl[:, k, :]), *ends)
                    else:
                        t = m - NK - QTILES
                        c = slice(P * t, P * t + P)
                        mm = three(ps[:, bank, 0:KVD], (xh[:, k, c], xl[:, k, c]), (wvh[:, k, :], wvl[:, k, :]), *ends)
                mm.then_inc(s_lat_units, 1)

            def scores(b, par, g):
                if g == 0:
                    pe.wait_ge(s_q_low, b + 1)
                    pe.wait_ge(s_keys, KDMA * (b + 1))
                q, k = qc[par], kt[par]
                for a in range(2):
                    mm = three(ps[:, B_S + a, 0:HALF],
                               [q[:, i, G * g:G * g + G, :].rearrange("p h s -> p (h s)") for i in range(2)],
                               [k[:, i, g, HALF * a:HALF * a + HALF] for i in range(2)], True, True)
                mm.then_inc(s_scores, 1)

            def wox_group(g):
                pe.wait_ge(s_out_split, g + 1)
                order = [(i, t) for i in range(OG) for t in range(TT)]
                if g == KV - 1:
                    order = [(i, t) for t in range(TT) for i in range(OG)]
                for i, t in order:
                    pe.wait_ge(s_wox_low, OG * g + i + 1)
                    c = slice(P * t, P * t + P)
                    last = g == KV - 1 and i == OG - 1
                    mm = three(ps[:, B_PROJ + t, :], (oh[:, g % 2, i, c], ol[:, g % 2, i, c]),
                               (hh[g % 2][:, i, :], hl[g % 2][:, i, :]), g == 0 and i == 0, last)
                    if last:
                        mm.then_inc(s_product, 1)
                if g < KV - 1:
                    mm.then_inc(s_wox_done, 1)

            tail_cuts = [cuts_of(B - 2)[-1], 26, 27, NU * KC]
            project(1, 1, 0, cuts_of(0)[0])
            scores(0, 0, 0)

            def attend(b, par):
                more = left(b) >= 1
                cuts = cuts_of(b)
                for g in range(KV):
                    n = KV * b + g
                    tail = not more and g == 0
                    if more:
                        project(b + 1, 1 - par, cuts[2 * g], cuts[2 * g + 1])
                    if tail:
                        project(b, par, tail_cuts[0], tail_cuts[1])
                    pe.wait_ge(s_probs, n + 1)
                    if not (is_first(b) and g == 0):
                        pe.wait_ge(s_probsT, n)
                        pe.wait_ge(s_probsT_lat, n)
                    for j in range(NV):
                        pe.transpose(ps[:, B_PT, P * j:P * j + P], pr[:, P * j:P * j + P], ident[:])
                    pe.transpose(ps[0:S, B_PT + 1, 0:P], pr[:, CTX:KEYS], ident[:]).then_inc(s_turned, 1)
                    if more:
                        project(b + 1, 1 - par, cuts[2 * g + 1], cuts[2 * g + 2])
                    if tail:
                        project(b, par, tail_cuts[1], tail_cuts[2])
                    if g + 1 < KV:
                        scores(b, par, g + 1)
                    elif more:
                        scores(b + 1, 1 - par, 0)
                    if tail:
                        project(b, par, tail_cuts[2], tail_cuts[3])
                    pe.wait_ge(s_probsT, n + 1)
                    pe.wait_ge(s_probsT_lat, n + 1)
                    if g == 0:
                        pe.wait_ge(s_v_out, NV * (b + 1) - 1)
                        pe.wait_ge(s_values_lat, 16 * (b + 1))
                    if not (is_first(b) and g < 2):
                        pe.wait_ge(s_placed, OPIECES * (n - 1))
                    o = ps[0:HD, B_O + g % 2, 0:P]
                    pe.matmul(o, vv[par][0:S, NV, HD * g:HD * g + HD], pt4[:], start=True, stop=False)
                    for j in range(NV):
                        if g == 0 and j == NV - 1:
                            pe.wait_ge(s_v_out, NV * (b + 1))
                        mm = pe.matmul(o, vv[par][:, j, HD * g:HD * g + HD], pt[:, P * j:P * j + P],
                                       start=False, stop=(j == NV - 1))
                    mm.then_inc(s_attended, 1)
                    if not more and g > 0:
                        wox_group(g - 1)

            each_batch(pe, attend)
            wox_group(KV - 1)

            def absorb(m, first=0, last=8):
                bank = B_S if m % 2 == 0 else B_O
                if m >= 2:
                    pe.wait_ge(s_absorbed_low, 2 * (m - 1))
                for i in range(first, last):
                    h = 8 * m + i
                    pe.matmul(ps[:, bank, KL * i:KL * i + KL], wqb[:, h, 0:P], wkn[:, h, :], start=True, stop=True)
                    mm = pe.matmul(ps[0:QB, bank + 1, KL * i:KL * i + KL], wqb[:, h, P:QL], wkn[:, h, :],
                                   start=True, stop=True)
                if last == 8:
                    mm.then_inc(s_absorbed, 1)

            pe.wait_ge(s_wqb, 32)
            pe.wait_ge(s_placed, OPIECES * KV * B)
            absorb(0)
            absorb(1, 0, 4)
            turn(1, B_PROJ)
            absorb(1, 4, 8)
            pe.wait_ge(s_wr, 32)
            pe.wait_ge(s_xnT, 2 * TT)
            for t in range(TT):
                for k in range(KC):
                    mm = pe.matmul(ps[:, B_PT + t, 0:LAT], xnT[:, k, P * t:P * t + P], wa[:, k, :],
                                   start=(k == 0), stop=(k == KC - 1))
                mm.then_inc(s_latents, 1)
            absorb(2)
            pe.wait_ge(s_normed, TT)
            for t in range(TT):
                pe.transpose(ps[:, B_PROJ, P * t:P * t + P], ql[:, t, 0:P], ident[:])
                tr = pe.transpose(ps[0:QB, B_PROJ, TOK + P * t:TOK + P * t + P], ql[:, t, P:QL], ident[:])
            tr.then_inc(s_latT, 1)
            absorb(3)
            pe.wait_ge(s_normed, TT + 2)
            for t in range(TT):
                tr = pe.transpose(ps[:, B_PROJ + 1, P * t:P * t + P], kp[:, t, :], ident[:])
            tr.then_inc(s_latT, 1)
            pe.wait_ge(s_absorbed_low, 4)
            pe.wait_ge(s_rope_low, 2)
            pe.wait_ge(s_latT_high, 3)
            pe.wait_ge(s_latT_low, 2)

            def copies(n):
                return 3 * (n // 2) + (3 if n % 2 else 2)

            def queries(lo, hi):
                for n in range(lo, hi):
                    if n == 1:
                        pe.wait_ge(s_latT_high, 4)
                    if n == 2:
                        pe.wait_ge(s_absorbed_low, 8)
                    if n >= 4:
                        pe.wait_ge(s_query_copies, copies(n - 4))
                        pe.wait_ge(s_rope_cos, n - 3)
                    for i in range(2):
                        h = 2 * n + i
                        o = ps[:, QBANK[n % 4], TOK * i:TOK * i + TOK]
                        three(o, (wqph[:, h, :], wqpl[:, h, :]), (qlah[:], qlal[:]), True, False)
                        pe.matmul(o, wqps[:, h, :], qlbh[:], start=False, stop=False)
                        mm = pe.matmul(o, wqps[0:QB, h, :], qlbl[:], start=False, stop=True)
                    mm.then_inc(s_queries, 1)

            def latent_scores(w, first=0, last=2):
                pe.wait_ge(s_query_copies, copies(4 * w + 3))
                pe.wait_ge(s_rope_sum, 4 * w + 4)
                for i in range(first, last):
                    for b in range(B):
                        g = 2 * w + i
                        mm = pe.matmul(ps[:, B_S + w, S * (B * i + b):S * (B * i + b) + S],
                                       qp[:, b, 4 * g:4 * g + 4, :].rearrange("p h s -> p (h s)"),
                                       kpT[:, S * b:S * b + S], start=True, stop=True)
                if last == 2:
                    mm.then_inc(s_mla_scores, 1)

            def combine(p):
                if p >= 2:
                    pe.wait_ge(s_combined_low, p if p in (6, 7) else 7 if p == 9 else p - 1)
                if p == 0:
                    pe.wait_ge(s_wvn, 16)
                if p % 4 == 0:
                    pe.wait_ge(s_wo[p // 4], 16)
                for odd in range(2):
                    h = 2 * p + odd
                    mm = pe.matmul(ps[KL * odd:KL * odd + KL, cbank(p), :], wvn[:, h, :], wo[h // 8][:, h % 8, :],
                                   start=True, stop=True)
                mm.then_inc(s_combined, 1)

            def turn_probs(w):
                pe.wait_ge(s_mla_probs, w + 1)
                if w >= 2:
                    pe.wait_ge(s_mla_probsT, w - 1)
                for t in range(TT):
                    for i in range(2):
                        at = B * S * i + P * t
                        tr = pe.transpose(ps[:, B_O + w % 2, P * (2 * t + i):P * (2 * t + i) + P],
                                          pm[:, w, at:at + P], ident[:])
                tr.then_inc(s_mla_turned, 1)

            def weighted(n):
                if n >= 4:
                    pe.wait_ge(s_weighted_low, 4 * n - 12)
                if n == 0:
                    pe.wait_ge(s_mla_probsT, 2)
                    pe.wait_ge(s_blockdiag, 4)
                if n == 2:
                    pe.wait_ge(s_mla_probsT, 4)
                tq, half = WEIGHTED[n]
                pe.matmul(ps[:, B_S + n % 4, :], bd[:, tq // 2, tq % 2, :], ptm[:, tq // 2, 4 * half:4 * half + 4, :],
                          start=True, stop=True).then_inc(s_weighted, 1)

            queries(0, 4)
            combine(0)
            queries(4, 6)
            combine(1)
            combine(2)
            queries(6, 8)
            latent_scores(0, 0, 1)
            combine(3)
            latent_scores(0, 1, 2)
            queries(8, 10)
            combine(4)
            queries(10, 12)
            latent_scores(1, 0, 1)
            combine(5)
            latent_scores(1, 1, 2)
            queries(12, 14)
            combine(6)
            pe.wait_ge(s_combined_low, 5)
            latent_scores(2, 0, 1)
            queries(14, 16)
            combine(7)
            latent_scores(2, 1, 2)
            combine(8)
            combine(9)
            pe.wait_ge(s_combined_low, 8)
            latent_scores(3, 0, 1)
            combine(10)
            latent_scores(3, 1, 2)
            turn_probs(0)
            turn_probs(1)
            combine(11)
            weighted(0)
            weighted(1)
            combine(12)
            turn_probs(2)
            combine(13)
            turn_probs(3)
            weighted(2)
            weighted(3)
            combine(14)
            combine(15)
            for n in range(4, 8):
                weighted(n)
            for t in range(TT):
                c = slice(P * t, P * t + P)
                pe.wait_ge(s_weighted_low, 16 * t + 16)
                for p in range(NPAIR):
                    if t == 1 and p == NPAIR - 3:
                        turn(2, B_PROJ, 0, 1)
                    pe.wait_ge(s_combined_low, p + 1)
                    w, at = wc[p // 4], 2 * (p % 4)
                    mm = three(ps[:, B_O + t, :], (och[:, p, c], ocl[:, p, c]), (w[:, at, :], w[:, at + 1, :]),
                               p == 0, p == NPAIR - 1)
                mm.then_inc(s_product, 1)
            pe.wait_ge(s_wf_exact, 1)
            for t in range(TT):
                c = slice(P * t, P * t + P)
                if t == 1:
                    turn(2, B_PROJ, 1, 2)
                pe.wait_ge(s_xnT, 2 * TT + t + 1)
                for half in (x3h, x3l):
                    if half is x3l:
                        pe.wait_ge(s_xnT_low, TT + t + 1)
                    for k in range(KC):
                        mm = pe.matmul(ps[:, B_S + t, :], half[:, k, c], wf[:, k, :],
                                       start=(k == 0 and half is x3h), stop=(k == KC - 1 and half is x3l))
                mm.then_inc(s_product, 1)


def lay_out(a):
    f = {k: np.ascontiguousarray(v) for k, v in a.items()}

    def chunks(w):
        return w.T.reshape(KC, P, w.shape[0]).transpose(1, 0, 2)

    def packed(w):
        w = np.concatenate([w[:, :OG], w[:, OG].reshape(KV, OG, HD // OG, D)], 2)
        return w.reshape(OT, P, D).transpose(1, 0, 2)

    turn = np.concatenate([np.arange(0, ROPE, 2), np.arange(1, ROPE, 2)])
    kva = f["L0_attn_wkv_a"]
    wqb = f["L0_attn_wq_b"].reshape(NH, NOPE + ROPE, QL)
    wkvb = f["L0_attn_wkv_b"].reshape(NH, NOPE + VD, KL)
    wqr = wqb[:, NOPE:, :][:, turn, :].transpose(2, 0, 1)
    freq = (1.0 / 10000.0 ** (np.arange(0, ROPE, 2, dtype=np.float32) / np.float32(ROPE))).astype(np.float32)
    ang = np.outer(np.arange(S, dtype=np.float32), freq).astype(np.float32)
    cos, sin = np.cos(ang).astype(np.float32), np.sin(ang).astype(np.float32)
    ropeq = np.zeros((P, 2, 32), np.float32)
    ropeq[KL:, 0, :] = np.concatenate([cos.T, cos.T])
    ropeq[KL:, 1, :] = np.concatenate([sin.T, -sin.T])
    big = np.finfo(np.float32)
    cap = np.where(np.tril(np.ones((S, S), bool)), big.max, big.min).astype(np.float32)
    d = {
        "x": f["x"].reshape(TOK, D),
        "ctxT": f["ctx_4096"].transpose(0, 2, 1).reshape(B, KC, P, CTX).transpose(0, 2, 1, 3),
        "wkT": chunks(f["L0_xattn_Wk"]), "wvT": chunks(f["L0_xattn_Wv"]), "wqT": chunks(f["L0_xattn_Wq"]),
        "woxT": packed(f["L0_xattn_Wo"].T.reshape(KV, G, HD, D)),
        "waT": chunks(np.concatenate([f["L0_attn_wq_a"], kva[:KL], kva[KL:][turn]])),
        "wqbn": wqb[:, :NOPE, :].transpose(1, 0, 2),
        "wqra": wqr[:P], "wqrb": wqr[P:],
        "wkn": wkvb[:, :NOPE, :].transpose(1, 0, 2),
        "wvn": wkvb[:, NOPE:, :].transpose(1, 0, 2),
        "wob": f["L0_attn_wo"].T.reshape(NH, VD, D).transpose(1, 0, 2),
        "wfT": chunks(f["L0_ffn_weight"]),
        "bias": f["L0_ffn_bias"].reshape(D), "qnw": f["L0_attn_q_norm_w"], "kvnw": f["L0_attn_kv_norm_w"],
        "ident": np.eye(P, dtype=np.float32),
        "ropek": np.tile(np.stack([cos, sin], 1), (4, 1, 1)), "ropeq": ropeq, "cap": np.tile(cap, (4, 1)),
    }
    return {k: np.ascontiguousarray(v) for k, v in d.items()}


def kernel(**inputs):
    from concourse import bacc
    from concourse.bass_utils import run_bass_kernel_spmd

    nc = bacc.Bacc("TRN2", target_bir_lowering=False, num_devices=1)
    arrays = lay_out({k: np.asarray(v) for k, v in inputs.items()})
    aps = {k: nc.dram_tensor("in_" + k, v.shape, mybir.dt.from_np(v.dtype), kind="ExternalInput").ap()
           for k, v in arrays.items()}
    out = nc.dram_tensor("out_0", (TOK, D), F32, kind="ExternalOutput").ap()
    build(nc, aps, out)
    r = run_bass_kernel_spmd(nc, [{"in_" + k: v for k, v in arrays.items()}], core_ids=[0])
    return r.results[0]["out_0"].reshape(B, S, D)
```
